# Optimizing a Trainium2 kernel written in Bass

```python
import numpy as np
import jax
import jax.numpy as jnp

def _softmax(x, axis=-1):
    return jax.nn.softmax(x, axis=axis)

def _gelu(x):
    return jax.nn.gelu(x, approximate=True)

def _silu(x):
    return jax.nn.silu(x)

def _sigmoid(x):
    return jax.nn.sigmoid(x)

def _layernorm(x, axis=-1, eps=1e-05):
    m = jnp.mean(x, axis=axis, keepdims=True)
    v = jnp.var(x, axis=axis, keepdims=True)
    return (x - m) / jnp.sqrt(v + eps)

def _scatter_add(tgt, idx, src, axis=0):
    return tgt.at[idx].add(src)

def _segment_sum(src, seg, n):
    return jax.ops.segment_sum(src, seg, n)
kernel_name = 'mk_macaron_d1_jaxref_r4_1f1334'

def setup_inputs(seed: int=0):
    np.random.seed(seed)
    _w = jnp.asarray

    def _L0_attn_setup():
        import jax, jax.numpy as jnp
        import numpy as np
        B, T, D, N = (8, 512, 256, 64)
        key = jax.random.key(seed)
        ks = jax.random.split(key, 6)
        sD = 1.0 / np.sqrt(D)
        sN = 1.0 / np.sqrt(N)
        return {'x': jax.random.normal(ks[0], (B, T, D), dtype=jnp.float32), 'Wa': jax.random.normal(ks[1], (D, N), dtype=jnp.float32) * sD, 'ba': jnp.zeros((N,), jnp.float32), 'Wb': jax.random.normal(ks[2], (D, N), dtype=jnp.float32) * sD, 'bb': jnp.zeros((N,), jnp.float32), 'Wc': jax.random.normal(ks[3], (D, N), dtype=jnp.float32) * sD, 'bc': jnp.zeros((N,), jnp.float32), 'Wd': jax.random.normal(ks[4], (D, D), dtype=jnp.float32) * sD, 'bd': jnp.zeros((D,), jnp.float32), 'Wy': jax.random.normal(ks[5], (N, D), dtype=jnp.float32) * sN, 'by': jnp.zeros((D,), jnp.float32)}
    _L0_attn_in = _L0_attn_setup()

    def _L0_ffn_setup():
        import jax, jax.numpy as jnp
        import numpy as np
        B, S, H, F, G = (8, 512, 256, 1024, 128)
        EPS = 1e-05

        def _dequant(q, scales, g):
            K, N = q.shape
            w = (q.astype(jnp.float32) - 128.0).reshape(K // g, g, N) * scales[:, None, :]
            return w.reshape(K, N)
        key = jax.random.key(seed)
        ks = jax.random.split(key, 8)
        x = jax.random.normal(ks[0], (B, S, H), dtype=jnp.float32)
        ln_gamma = jnp.ones((H,), jnp.float32)
        ln_beta = jnp.zeros((H,), jnp.float32)
        fc1_q = jax.random.randint(ks[1], (H, F), 0, 64, dtype=jnp.int32)
        fc2_q = jax.random.randint(ks[2], (F, H), 0, 64, dtype=jnp.int32)
        fc1_scales = jax.random.uniform(ks[3], (H // G, F), jnp.float32) * 0.02 + 0.001
        fc2_scales = jax.random.uniform(ks[4], (F // G, H), jnp.float32) * 0.02 + 0.001
        fc1_bias = jax.random.normal(ks[5], (F,), jnp.float32) * 0.02
        fc2_bias = jax.random.normal(ks[6], (H,), jnp.float32) * 0.02
        return {'x': x, 'ln_gamma': ln_gamma, 'ln_beta': ln_beta, 'fc1_q': fc1_q, 'fc1_scales': fc1_scales, 'fc1_bias': fc1_bias, 'fc2_q': fc2_q, 'fc2_scales': fc2_scales, 'fc2_bias': fc2_bias}
    _L0_ffn_in = _L0_ffn_setup()
    _d = {'L0_attn_x': _L0_attn_in['x'], 'L0_attn_Wa': _L0_attn_in['Wa'], 'L0_attn_ba': _L0_attn_in['ba'], 'L0_attn_Wb': _L0_attn_in['Wb'], 'L0_attn_bb': _L0_attn_in['bb'], 'L0_attn_Wc': _L0_attn_in['Wc'], 'L0_attn_bc': _L0_attn_in['bc'], 'L0_attn_Wd': _L0_attn_in['Wd'], 'L0_attn_bd': _L0_attn_in['bd'], 'L0_attn_Wy': _L0_attn_in['Wy'], 'L0_attn_by': _L0_attn_in['by'], 'L0_ffn_ln_gamma': _L0_ffn_in['ln_gamma'], 'L0_ffn_ln_beta': _L0_ffn_in['ln_beta'], 'L0_ffn_fc1_q': _L0_ffn_in['fc1_q'], 'L0_ffn_fc1_scales': _L0_ffn_in['fc1_scales'], 'L0_ffn_fc1_bias': _L0_ffn_in['fc1_bias'], 'L0_ffn_fc2_q': _L0_ffn_in['fc2_q'], 'L0_ffn_fc2_scales': _L0_ffn_in['fc2_scales'], 'L0_ffn_fc2_bias': _L0_ffn_in['fc2_bias']}
    _x0 = _d['L0_attn_x']
    _d['L0_attn_x'] = jax.random.normal(jax.random.fold_in(jax.random.key(seed), 1), (8, 1024, 256), dtype=_x0.dtype)
    del _x0
    return _d

def reference(L0_attn_x, L0_attn_Wa, L0_attn_ba, L0_attn_Wb, L0_attn_bb, L0_attn_Wc, L0_attn_bc, L0_attn_Wd, L0_attn_bd, L0_attn_Wy, L0_attn_by, L0_ffn_ln_gamma, L0_ffn_ln_beta, L0_ffn_fc1_q, L0_ffn_fc1_scales, L0_ffn_fc1_bias, L0_ffn_fc2_q, L0_ffn_fc2_scales, L0_ffn_fc2_bias):

    def _L0_attn_ref(x, Wa, ba, Wb, bb, Wc, bc, Wd, bd, Wy, by):
        import jax, jax.numpy as jnp
        import numpy as np
        B, T, D, N = (8, 512, 256, 64)
        a = jax.nn.sigmoid(jnp.einsum('btd,dn->btn', x, Wa) + ba)
        b = jnp.einsum('btd,dn->btn', x, Wb) + bb
        c = jnp.tanh(jnp.einsum('btd,dn->btn', x, Wc) + bc)
        d = jnp.einsum('btd,de->bte', x, Wd) + bd

        def step(s, abc):
            at, bt, ct = abc
            s = at * s + (1.0 - at) * bt
            return (s, ct * s)
        aT = jnp.swapaxes(a, 0, 1)
        bT = jnp.swapaxes(b, 0, 1)
        cT = jnp.swapaxes(c, 0, 1)
        s0 = jnp.zeros((x.shape[0], Wa.shape[1]), x.dtype)
        _, csT = jax.lax.scan(step, s0, (aT, bT, cT))
        cs = jnp.swapaxes(csT, 0, 1)
        y = jnp.einsum('btn,nd->btd', cs, Wy) + by + d
        return y

    def _L0_ffn_ref(x, ln_gamma, ln_beta, fc1_q, fc1_scales, fc1_bias, fc2_q, fc2_scales, fc2_bias):
        import jax, jax.numpy as jnp
        import numpy as np
        B, S, H, F, G = (8, 512, 256, 1024, 128)
        EPS = 1e-05

        def _dequant(q, scales, g):
            K, N = q.shape
            w = (q.astype(jnp.float32) - 128.0).reshape(K // g, g, N) * scales[:, None, :]
            return w.reshape(K, N)
        residual = x
        mu = jnp.mean(x, axis=-1, keepdims=True)
        var = jnp.mean(jnp.square(x - mu), axis=-1, keepdims=True)
        h = (x - mu) * jax.lax.rsqrt(var + EPS) * ln_gamma + ln_beta
        hf = h.reshape(-1, H)
        w1 = _dequant(fc1_q, fc1_scales, G)
        y = hf @ w1 + fc1_bias
        y = jax.nn.silu(y)
        w2 = _dequant(fc2_q, fc2_scales, G)
        z = y @ w2 + fc2_bias
        return residual + 0.5 * z.reshape(residual.shape)
    x = L0_attn_x
    x = x + 0.5 * _L0_ffn_ref(_layernorm(x, axis=-1), L0_ffn_ln_gamma, L0_ffn_ln_beta, L0_ffn_fc1_q, L0_ffn_fc1_scales, L0_ffn_fc1_bias, L0_ffn_fc2_q, L0_ffn_fc2_scales, L0_ffn_fc2_bias)
    x = x + _L0_attn_ref(_layernorm(x, axis=-1), L0_attn_Wa, L0_attn_ba, L0_attn_Wb, L0_attn_bb, L0_attn_Wc, L0_attn_bc, L0_attn_Wd, L0_attn_bd, L0_attn_Wy, L0_attn_by)
    x = x + 0.5 * _L0_ffn_ref(_layernorm(x, axis=-1), L0_ffn_ln_gamma, L0_ffn_ln_beta, L0_ffn_fc1_q, L0_ffn_fc1_scales, L0_ffn_fc1_bias, L0_ffn_fc2_q, L0_ffn_fc2_scales, L0_ffn_fc2_bias)
    return x

_drawn_inputs = setup_inputs


def setup_inputs(seed=0):
    import zlib

    import numpy as np

    out = dict(_drawn_inputs(seed))
    spreads = {'L0_attn_ba': (0.0, 2.0),
     'L0_attn_bb': (0.0, 2.0),
     'L0_attn_bc': (0.0, 2.0),
     'L0_attn_bd': (0.0, 2.0),
     'L0_attn_by': (0.0, 2.0),
     'L0_ffn_ln_gamma': (1.0, 0.2),
     'L0_ffn_ln_beta': (0.0, 0.1)}
    factors = {'L0_attn_Wa': 8.0,
     'L0_attn_Wb': 8.0,
     'L0_attn_Wc': 8.0,
     'L0_attn_Wd': 61.685,
     'L0_attn_Wy': 8.0,
     'L0_ffn_fc1_bias': 60.275,
     'L0_ffn_fc2_bias': 200.0}
    for name, (base, spread) in spreads.items():
        noise = np.random.default_rng([zlib.crc32(name.encode()), seed]).standard_normal(out[name].shape)
        drawn = base * np.exp(spread * noise) if base else spread * noise
        out[name] = jnp.asarray(drawn.astype(out[name].dtype))
    for name, factor in factors.items():
        out[name] = (out[name] * factor).astype(out[name].dtype)
    return out
```

```python
from contextlib import ExitStack

import concourse.bass as bass
from concourse import mybir

ALU = mybir.AluOpType
ACT = mybir.ActivationFunctionType
F32 = mybir.dt.float32
F32R = mybir.dt.float32r
I32 = mybir.dt.int32

P = 128
TILE = 512
SUB = TILE // P
LAG = 3
EPS = 1e-5
ZERO_POINT = 128.0


def macaron_kernel(nc, x, wa, ba, wb, bb, wc, bc, wd, bd, wy, by, gamma, beta,
                   q1, s1, b1, q2, s2, b2, out):
    B, S, D = x.shape
    N = wa.shape[1]
    F = q1.shape[1]
    NT = B * S // TILE
    KC = D // P
    FC = F // P
    PAIRS = (NT - 4) // 2
    assert KC == 2 and 2 * N == P and S == 2 * TILE and FC == 8 and NT % 2 == 0
    assert s1.shape[0] == KC and s2.shape[0] == FC

    x_view = x.rearrange("b s d -> (b s) d").rearrange("(t a p) d -> p t a d", p=P, a=SUB)
    out_view = out.rearrange("b s d -> (b s) d").rearrange("(t a p) d -> p t a d", p=P, a=SUB)

    R_S1, R_B1 = 0, KC * FC
    R_S2 = R_B1 + FC
    R_B2 = R_S2 + FC * KC
    R_GAMMA = R_B2 + KC
    R_BETA = R_GAMMA + KC
    R_AB = R_BETA + KC
    R_C = R_AB + 1
    ROWS = R_C + 1

    with ExitStack() as ctx:
        def sb(name, shape, dt=F32):
            return ctx.enter_context(nc.sbuf_tensor(name, shape, dt))

        def sem(name):
            return ctx.enter_context(nc.semaphore(name))

        resid = sb("resid", [P, NT, SUB, D])
        q1_int = sb("q1_int", [P, KC, F], I32)
        q2_int = sb("q2_int", [P, FC, D], I32)
        q1_sb = sb("q1_sb", [P, KC, F], F32R)
        q2_sb = sb("q2_sb", [P, FC, D], F32R)
        wab_sb = sb("wab_sb", [P, KC, 2 * N])
        wc_sb = sb("wc_sb", [P, KC, N])
        wd_sb = sb("wd_sb", [P, KC, D])
        wy_sb = sb("wy_sb", [N + 1, D])
        bias_rows = sb("bias_rows", [N + 1, 2, D])
        rows = sb("rows", [ROWS, P])
        cols = sb("cols", [P, ROWS])
        ident = sb("ident", [P, P])
        minus_half = sb("minus_half", [P, 2 * SUB])
        stats = sb("stats", [P, SUB, 6])
        mean_var = sb("mean_var", [P, SUB, 2])
        var_terms = sb("var_terms", [P, 2 * SUB])
        rstd = sb("rstd", [P, 2 * SUB])
        res_scale = sb("res_scale", [P, SUB])
        res_shift = sb("res_shift", [P, SUB])
        wait_holder = sb("wait_holder", [P, 1])
        xhat = sb("xhat", [P, SUB, D])
        h_full = sb("h_full", [P, KC, TILE])
        h_hi = sb("h_hi", [P, 2, KC, TILE], F32R)
        h_lo = sb("h_lo", [P, 2, KC, TILE], F32R)
        u_sb = sb("u_sb", [P, 2, TILE])
        y_sb = sb("y_sb", [P, 2, TILE])
        g_full = sb("g_full", [P, 2, TILE])
        g_hi = sb("g_hi", [P, 4, TILE], F32R)
        g_lo = sb("g_lo", [P, 4, TILE], F32R)
        z_acc = sb("z_acc", [P, 2, KC, TILE])
        xn = sb("xn", [P, 2, KC, TILE])
        a_sb = sb("a_sb", [N, 2, TILE])
        b_sb = sb("b_sb", [N, 2, TILE])
        c_sb = sb("c_sb", [N, 2, TILE])
        drive = sb("drive", [N, 2, TILE])
        state = sb("state", [N, 2, TILE])
        cs_sb = sb("cs_sb", [N + 1, 2, TILE])

        ps_fc1 = ctx.enter_context(nc.psum_tensor("ps_fc1", [P, 2, KC, TILE], F32))
        ps_z = ctx.enter_context(nc.psum_tensor("ps_z", [P, KC, TILE], F32))
        ps_tr = ctx.enter_context(nc.psum_tensor("ps_tr", [P, TILE], F32))
        ps_back = ctx.enter_context(nc.psum_tensor("ps_back", [P, TILE], F32))
        ps_ab = ps_z[:, 0, :]
        ps_c = ps_z[0:N, 1, :]
        ps_mix = ps_fc1

        x_loaded = [sem("x_loaded_even"), sem("x_loaded_odd")]
        rows_zero = sem("rows_zero")
        rows_loaded = sem("rows_loaded")
        q1_loaded = sem("q1_loaded")
        q2_loaded = sem("q2_loaded")
        mixer_loaded = sem("mixer_loaded")
        ident_zero = sem("ident_zero")
        consts_ready = sem("consts_ready")
        rows_turned = sem("rows_turned")
        cols_ready = sem("cols_ready")
        q1_ready = sem("q1_ready")
        q2_ready = sem("q2_ready")
        mixer_ready = sem("mixer_ready")
        stored = sem("stored")
        stats_done = sem("stats_done")
        aggr_done = sem("aggr_done")
        var_ready = sem("var_ready")
        rstd_ready = sem("rstd_ready")
        res_terms = sem("res_terms")
        xhat_ready = sem("xhat_ready")
        resid_scaled = sem("resid_scaled")
        turned = sem("turned")
        turned_out = sem("turned_out")
        h_hi_ready = sem("h_hi_ready")
        h_ready = sem("h_ready")
        fc1_done = sem("fc1_done")
        u_ready = sem("u_ready")
        y_ready = sem("y_ready")
        g_hi_ready = sem("g_hi_ready")
        g_ready = sem("g_ready")
        fc2_done = sem("fc2_done")
        z_added = sem("z_added")
        back_done = sem("back_done")
        ffn_added = sem("ffn_added")
        ab_done = sem("ab_done")
        c_done = sem("c_done")
        a_ready = sem("a_ready")
        b_ready = sem("b_ready")
        c_ready = sem("c_ready")
        drive_ready = sem("drive_ready")
        state_ready = sem("state_ready")
        cs_ready = sem("cs_ready")
        mix_done = sem("mix_done")
        mix_added = sem("mix_added")

        def col(r):
            return cols[:, r:r + 1]

        def wait(eng, signal, count):
            if type(count) is not int or count > 0:
                eng.wait_ge(signal, count)

        def over_tiles(eng, tile):
            tile(0, 0, False, True)
            tile(1, 1, True, True)
            with eng.Fori(0, PAIRS) as i:
                tile(2 * i + 2, 0, True, True)
                tile(2 * i + 3, 1, True, True)
            tile(NT - 2, 0, True, True)
            tile(NT - 1, 1, True, False)

        block = ctx.enter_context(nc.Block())

        @block.sync
        def _(sp):
            sp.wait_ge(rows_zero, 1)
            small = [(s1.rearrange("k (c p) -> (k c) p", p=P), R_S1, KC * FC),
                     (b1.rearrange("(c p) -> c p", p=P), R_B1, FC),
                     (s2.rearrange("g (n p) -> (g n) p", p=P), R_S2, FC * KC),
                     (b2.rearrange("(n p) -> n p", p=P), R_B2, KC),
                     (gamma.rearrange("(k p) -> k p", p=P), R_GAMMA, KC),
                     (beta.rearrange("(k p) -> k p", p=P), R_BETA, KC)]
            sp.dma_start(resid[:, 0, :, :], x_view[:, 0, :, :]).then_inc(x_loaded[0], 16)
            for src, r, n in small:
                sp.dma_start(rows[r:r + n, :], src).then_inc(rows_loaded, 16)
            for v, r, at in ((ba, R_AB, 0), (bb, R_AB, N), (bc, R_C, 0)):
                sp.dma_start(rows[r:r + 1, at:at + N], v.rearrange("(a n) -> a n", a=1)).then_inc(rows_loaded, 16)
            sp.dma_start(resid[:, 1, :, :], x_view[:, 1, :, :]).then_inc(x_loaded[1], 16)
            with sp.Fori(0, NT // 2 - 1) as i:
                for par in range(2):
                    sp.wait_ge(x_loaded[par], 16 * i + 16)
                    sp.dma_start(resid[:, 2 * i + (2 + par), :, :],
                                 x_view[:, 2 * i + (2 + par), :, :]).then_inc(x_loaded[par], 16)

            with sp.Fori(0, NT) as t:
                sp.wait_ge(ffn_added, 2 * t + (2 * NT + 2))
                sp.dma_start(out_view[:, t, :, :], resid[:, t, :, :]).then_inc(stored, 16)
            sp.wait_ge(stored, 16 * NT)

        @block.gpsimd
        def _(pool):
            nc.gpsimd.memset(rows[:, :], 0.0).then_inc(rows_zero, 1)
            nc.gpsimd.memset(ident[:, :], 0.0).then_inc(ident_zero, 1)
            pool.wait_ge(ident_zero, 1)
            nc.gpsimd.affine_select(out=ident[:, :], in_=ident[:, :], compare_op=ALU.not_equal, fill=1.0,
                                    base=0, pattern=[[-1, P]], channel_multiplier=1).then_inc(consts_ready, 1)
            pool.wait_ge(consts_ready, 1)
            nc.gpsimd.memset(cs_sb[N:N + 1, :, :], 1.0).then_inc(consts_ready, 1)
            pool.wait_ge(consts_ready, 2)
            nc.gpsimd.memset(minus_half[:, :], -0.5).then_inc(consts_ready, 1)
            pool.wait_ge(consts_ready, 3)

            def rsqrt(ln, n):
                pool.wait_ge(var_ready, ln + 1)
                nc.gpsimd.tensor_tensor(rstd[:, 0:n], var_terms[:, 0:n], minus_half[:, 0:n],
                                        ALU.pow).then_inc(rstd_ready, 1)

            def h_low(ff, par, c):
                pool.wait_ge(h_hi_ready, 2 * ff + (c + 1))
                wait(pool, fc1_done, FC * ff - FC)
                nc.gpsimd.tensor_tensor(h_lo[:, par, c, :], h_full[:, c, :], h_hi[:, par, c, :].bitcast(F32),
                                        ALU.subtract).then_inc(h_ready, 1)

            def g_low(step, slot):
                pool.wait_ge(g_hi_ready, step + 1)
                wait(pool, fc2_done, 2 * step - 6)
                nc.gpsimd.tensor_tensor(g_lo[:, slot % 4, :], g_full[:, slot % 2, :],
                                        g_hi[:, slot % 4, :].bitcast(F32), ALU.subtract).then_inc(g_ready, 1)

            def feed_forward(ff0, ln0):
                def tile(t, par, before, behind):
                    ff, ln = t + ff0, t + ln0
                    for f in range(FC):
                        if before or f >= 1:
                            g_low(FC * ff + (f - 1), f + 7)
                        if behind:
                            if f == 0:
                                rsqrt(ln + 1, 2 * SUB)
                            if f in (4, 5):
                                h_low(ff + 1, 1 - par, f - 4)
                rsqrt(ln0, 2 * SUB)
                for c in range(KC):
                    h_low(ff0, 0, c)
                over_tiles(pool, tile)
                g_low(FC * (ff0 + NT) - 1, 7)

            feed_forward(0, 0)

            def mixer_tile(t, par, before, behind):
                if behind:
                    rsqrt(t + (NT + 1), SUB)
            rsqrt(NT, SUB)
            over_tiles(pool, mixer_tile)

            feed_forward(NT, 2 * NT)

        @block.scalar
        def _(act):
            act.dma_start(q1_int[:, :, :], q1.rearrange("(k p) f -> p k f", p=P)).then_inc(q1_loaded, 16)
            act.dma_start(q2_int[:, :, :], q2.rearrange("(g p) d -> p g d", p=P)).then_inc(q2_loaded, 16)
            for dst, src in ((wab_sb[:, :, 0:N], wa), (wab_sb[:, :, N:2 * N], wb), (wc_sb[:, :, :], wc),
                             (wd_sb[:, :, :], wd)):
                act.dma_start(dst, src.rearrange("(k p) n -> p k n", p=P)).then_inc(mixer_loaded, 16)
            act.dma_start(wy_sb[0:N, :], wy).then_inc(mixer_loaded, 16)
            for i, v in enumerate((by, bd)):
                act.dma_start(bias_rows[N:N + 1, i, :], v.rearrange("(a n) -> a n", a=1)).then_inc(mixer_loaded, 16)
            act.wait_ge(rows_turned, 1)
            nc.scalar.activation(cols[:, :], ps_back[:, 0:ROWS], ACT.Copy).then_inc(cols_ready, 1)
            act.wait_ge(cols_ready, 1)

            def affine(ln, ff, c):
                act.wait_ge(turned, 2 * ln + (c + 1))
                wait(act, h_ready, 2 * ff + (c - 1))
                nc.scalar.activation(h_full[:, c, :], ps_tr[:, :], ACT.Identity, bias=col(R_BETA + c),
                                     scale=col(R_GAMMA + c)).then_inc(turned_out, 1)

            def first_group(step, f):
                act.wait_ge(fc1_done, step + 1)
                wait(act, y_ready, step - 1)
                nc.scalar.activation(u_sb[:, f % 2, :], ps_fc1[:, f % 2, 0, :], ACT.Identity,
                                     bias=col(R_B1 + f), scale=col(R_S1 + f)).then_inc(u_ready, 1)

            def silu(step, slot):
                act.wait_ge(y_ready, step + 1)
                wait(act, g_ready, step - 1)
                nc.scalar.activation(g_full[:, slot % 2, :], y_sb[:, slot % 2, :], ACT.Silu)
                wait(act, fc2_done, 2 * step - 6)
                nc.scalar.activation(g_hi[:, slot % 4, :], y_sb[:, slot % 2, :],
                                     ACT.Silu).then_inc(g_hi_ready, 1)

            def feed_forward(ff0, ln0):
                def tile(t, par, before, behind):
                    ff, ln = t + ff0, t + ln0
                    for f in range(FC):
                        first_group(FC * ff + f, f)
                        if before or f >= 1:
                            silu(FC * ff + (f - 1), f + 7)
                        if behind and f in (3, 4):
                            affine(ln + 1, ff + 1, f - 3)
                for c in range(KC):
                    affine(ln0, ff0, c)
                over_tiles(act, tile)
                silu(FC * (ff0 + NT) - 1, 7)

            feed_forward(0, 0)

            def turn_out(t, par, c):
                act.wait_ge(turned, 2 * t + (2 * NT + c + 1))
                wait(act, mix_done, 2 * t - 2)
                nc.scalar.activation(xn[:, par, c, :], ps_tr[:, :], ACT.Copy).then_inc(turned_out, 1)

            def mixer_tile(t, par, before, behind):
                act.wait_ge(ab_done, t + 1)
                wait(act, cs_ready, t)
                nc.scalar.activation(a_sb[:, par, :], ps_ab[0:N, :], ACT.Sigmoid,
                                     bias=cols[0:N, R_AB:R_AB + 1]).then_inc(a_ready, 1)
                nc.scalar.activation(b_sb[:, par, :], ps_ab[N:2 * N, :], ACT.Identity,
                                     bias=cols[N:2 * N, R_AB:R_AB + 1]).then_inc(b_ready, 1)
                act.wait_ge(c_done, t + 1)
                nc.scalar.activation(c_sb[:, par, :], ps_c, ACT.Tanh,
                                     bias=cols[0:N, R_C:R_C + 1]).then_inc(c_ready, 1)
                if behind:
                    for c in range(KC):
                        turn_out(t + 1, 1 - par, c)
            for c in range(KC):
                turn_out(0, 0, c)
            over_tiles(act, mixer_tile)

            feed_forward(NT, 2 * NT)

        @block.vector
        def _(dve):
            dve.wait_ge(q1_loaded, 16)
            nc.vector.tensor_scalar(q1_sb[:, :, :], q1_int[:, :, :], -ZERO_POINT, None, ALU.add).then_inc(q1_ready, 1)
            dve.wait_ge(q2_loaded, 16)
            nc.vector.tensor_scalar(q2_sb[:, :, :], q2_int[:, :, :], -ZERO_POINT, None, ALU.add).then_inc(q2_ready, 1)
            dve.wait_ge(mixer_loaded, 16 * 7)
            nc.vector.tensor_tensor(wy_sb[N:N + 1, :], bias_rows[N:N + 1, 0, :], bias_rows[N:N + 1, 1, :],
                                    ALU.add).then_inc(mixer_ready, 1)
            dve.wait_ge(cols_ready, 1)

            def variance(ln, t, twice):
                for a in range(SUB):
                    last = nc.vector.bn_stats(stats[:, a, :], resid[:, t, a, :])
                last.then_inc(stats_done, 1)
                dve.wait_ge(stats_done, ln + 1)
                nc.vector.memset(wait_holder[:, :], 0.0)
                for a in range(SUB):
                    last = nc.vector.bn_aggr(mean_var[:, a, :], stats[:, a, :])
                last.then_inc(aggr_done, 1)
                dve.wait_ge(aggr_done, ln + 1)
                last = nc.vector.tensor_scalar(var_terms[:, 0:SUB], mean_var[:, :, 1], EPS, None, ALU.add)
                if twice:
                    last = nc.vector.tensor_scalar(var_terms[:, SUB:2 * SUB], mean_var[:, :, 1], 1.0 + EPS,
                                                   EPS * EPS, ALU.mult, ALU.add)
                last.then_inc(var_ready, 1)

            def normalise(ln, t, twice):
                dve.wait_ge(rstd_ready, ln + 1)
                wait(dve, turned, 2 * ln)
                at = SUB if twice else 0
                for a in range(SUB):
                    last = nc.vector.tensor_scalar(xhat[:, a, :], resid[:, t, a, :], mean_var[:, a, 0:1],
                                                   rstd[:, at + a:at + a + 1], ALU.subtract, ALU.mult)
                last.then_inc(xhat_ready, 1)

            def residual(ln, ff, t):
                nc.vector.tensor_scalar(res_scale[:, :], rstd[:, 0:SUB], 0.5, 1.0, ALU.mult, ALU.add)
                nc.vector.scalar_tensor_tensor(out=res_shift[:, :], in0=mean_var[:, :, 0], scalar=-0.5,
                                               in1=rstd[:, 0:SUB], op0=ALU.mult, op1=ALU.mult).then_inc(res_terms, 1)
                dve.wait_ge(res_terms, ff + 1)
                for a in range(SUB):
                    last = nc.vector.tensor_scalar(resid[:, t, a, :], resid[:, t, a, :], res_scale[:, a:a + 1],
                                                   res_shift[:, a:a + 1], ALU.mult, ALU.add)
                last.then_inc(resid_scaled, 1)

            def h_high(ln, ff, par, c):
                dve.wait_ge(turned_out, 2 * ln + (c + 1))
                wait(dve, fc1_done, FC * ff - FC)
                nc.vector.tensor_copy(h_hi[:, par, c, :], h_full[:, c, :]).then_inc(h_hi_ready, 1)

            def second_group(step, f):
                dve.wait_ge(u_ready, step + 1)
                wait(dve, g_hi_ready, step - 1)
                nc.vector.scalar_tensor_tensor(out=y_sb[:, f % 2, :], in0=ps_fc1[:, f % 2, 1, :],
                                               scalar=col(R_S1 + FC + f), in1=u_sb[:, f % 2, :],
                                               op0=ALU.mult, op1=ALU.add).then_inc(y_ready, 1)

            def add_group(step, ff, g, par):
                for n in range(KC):
                    dve.wait_ge(fc2_done, 2 * step + (n + 1))
                    r = R_S2 + KC * g + n
                    if g == 0:
                        wait(dve, back_done, 2 * ff - 2)
                        op = nc.vector.tensor_scalar(z_acc[:, par, n, :], ps_z[:, n, :], col(r), col(R_B2 + n),
                                                     ALU.mult, ALU.add)
                    else:
                        dve.wait_ge(z_added, 2 * step + (n - 1))
                        op = nc.vector.scalar_tensor_tensor(out=z_acc[:, par, n, :], in0=ps_z[:, n, :],
                                                            scalar=col(r), in1=z_acc[:, par, n, :],
                                                            op0=ALU.mult, op1=ALU.add)
                    op.then_inc(z_added, 1)

            def add_ffn(ff, t, half):
                dve.wait_ge(back_done, 2 * ff + (half + 1))
                dve.wait_ge(resid_scaled, ff + 1)
                part = resid[:, t, 2 * half:2 * half + 2, :]
                nc.vector.scalar_tensor_tensor(out=part, in0=ps_back[:, :].rearrange("p (a d) -> p a d", a=2),
                                               scalar=0.25, in1=part, op0=ALU.mult,
                                               op1=ALU.add).then_inc(ffn_added, 1)

            def feed_forward(ff0, ln0):
                def tile(t, par, before, behind):
                    ff, ln = t + ff0, t + ln0
                    for f in range(FC):
                        second_group(FC * ff + f, f)
                        if before or f >= LAG:
                            g = (f - LAG) % FC
                            if f >= LAG:
                                add_group(FC * ff + (f - LAG), ff, g, par)
                            else:
                                add_group(FC * ff + (f - LAG), ff - 1, g, 1 - par)
                        if behind:
                            if f == 0:
                                if ff0 == 0:
                                    loaded_wait(t, par)
                                variance(ln + 1, t + 1, True)
                            if f == 1:
                                normalise(ln + 1, t + 1, True)
                            if f == 2:
                                residual(ln + 1, ff + 1, t + 1)
                            if f in (4, 5):
                                h_high(ln + 1, ff + 1, 1 - par, f - 4)
                        if before and f in (5, 7):
                            add_ffn(ff - 1, t - 1, (f - 5) // 2)

                def loaded_wait(t, par):
                    dve.wait_ge(x_loaded[1 - par], 8 * t + (16 if par == 0 else 24))

                if ff0 == 0:
                    dve.wait_ge(x_loaded[0], 16)
                variance(ln0, 0, True)
                normalise(ln0, 0, True)
                residual(ln0, ff0, 0)
                for c in range(KC):
                    h_high(ln0, ff0, 0, c)
                over_tiles(dve, tile)
                end = ff0 + NT
                for f in range(LAG):
                    add_group(FC * end + f - LAG, end - 1, FC + f - LAG, 1)
                for half in range(2):
                    add_ffn(end - 1, NT - 1, half)

            feed_forward(0, 0)

            def scan(t, par):
                dve.wait_ge(b_ready, t + 1)
                nc.vector.scalar_tensor_tensor(out=drive[:, par, :], in0=a_sb[:, par, :], scalar=1.0,
                                               in1=b_sb[:, par, :], op0=ALU.subtract,
                                               op1=ALU.mult).then_inc(drive_ready, 1)
                dve.wait_ge(drive_ready, t + 1)
                nc.vector.tensor_tensor_scan(state[:, par, :], a_sb[:, par, :], drive[:, par, :],
                                             state[:, 0, TILE - 1:TILE] if par else 0.0,
                                             ALU.mult, ALU.subtract).then_inc(state_ready, 1)
                dve.wait_ge(state_ready, t + 1)
                dve.wait_ge(c_ready, t + 1)
                wait(dve, mix_done, 2 * t - 2)
                nc.vector.tensor_tensor(cs_sb[0:N, par, :], c_sb[:, par, :], state[:, par, :],
                                        ALU.mult).then_inc(cs_ready, 1)

            def add_mixer(t, par, half):
                dve.wait_ge(mix_done, 2 * t + (half + 1))
                part = resid[:, t, 2 * half:2 * half + 2, :]
                nc.vector.tensor_tensor(part, ps_mix[:, par, half, :].rearrange("p (a d) -> p a d", a=2), part,
                                        ALU.add).then_inc(mix_added, 1)

            def mixer_tile(t, par, before, behind):
                if behind:
                    variance(t + (NT + 1), t + 1, False)
                    normalise(t + (NT + 1), t + 1, False)
                scan(t, par)
                for half in range(2):
                    add_mixer(t, par, half)

            variance(NT, 0, False)
            normalise(NT, 0, False)
            over_tiles(dve, mixer_tile)

            dve.wait_ge(mix_added, 2 * NT)
            feed_forward(NT, 2 * NT)

        @block.tensor
        def _(pe):
            pe.wait_ge(consts_ready, 3)
            pe.wait_ge(rows_loaded, 16 * 9)
            nc.tensor.transpose(ps_back[:, 0:ROWS], rows[:, :], ident[0:ROWS, 0:ROWS]).then_inc(rows_turned, 1)

            def turn(ln, c):
                pe.wait_ge(xhat_ready, ln + 1)
                wait(pe, turned_out, 2 * ln + c)
                for a in range(SUB):
                    last = nc.tensor.transpose(ps_tr[:, a * P:(a + 1) * P], xhat[:, a, c * P:(c + 1) * P],
                                               ident[:, :])
                last.then_inc(turned, 1)

            def fc1(step, ff, f, par):
                if f == 0:
                    pe.wait_ge(h_ready, 2 * ff + 2)
                wait(pe, y_ready, step - 1)
                for k in range(KC):
                    for part in (h_hi, h_lo):
                        last = nc.tensor.matmul(ps_fc1[:, f % 2, k, :], q1_sb[:, k, f * P:(f + 1) * P],
                                                part[:, par, k, :], start=part is h_hi, stop=part is h_lo)
                last.then_inc(fc1_done, 1)

            def fc2(step, g):
                pe.wait_ge(g_ready, step + 1)
                for n in range(KC):
                    wait(pe, z_added, 2 * step + (n - 1))
                    for part in (g_hi, g_lo):
                        last = nc.tensor.matmul(ps_z[:, n, :], q2_sb[:, g, n * P:(n + 1) * P],
                                                part[:, g % 4, :], start=part is g_hi, stop=part is g_lo)
                    last.then_inc(fc2_done, 1)

            def turn_back(ff, par, half):
                pe.wait_ge(z_added, 16 * ff + 16)
                wait(pe, ffn_added, 2 * ff + half)
                for a in range(2):
                    at = (2 * half + a) * P
                    for n in range(KC):
                        last = nc.tensor.transpose(ps_back[:, a * D + n * P:a * D + (n + 1) * P],
                                                   z_acc[:, par, n, at:at + P], ident[:, :])
                last.then_inc(back_done, 1)

            def feed_forward(ff0, ln0):
                def tile(t, par, before, behind):
                    ff, ln = t + ff0, t + ln0
                    for f in range(FC):
                        fc1(FC * ff + f, ff, f, par)
                        if before or f >= LAG:
                            fc2(FC * ff + (f - LAG), (f - LAG) % FC)
                        if behind and f in (2, 3):
                            turn(ln + 1, f - 2)
                        if before and f in (4, 6):
                            turn_back(ff - 1, 1 - par, (f - 4) // 2)
                for c in range(KC):
                    turn(ln0, c)
                if ff0 == 0:
                    pe.wait_ge(cols_ready, 1)
                    pe.wait_ge(q1_ready, 1)
                    pe.wait_ge(q2_ready, 1)
                over_tiles(pe, tile)
                end = ff0 + NT
                for f in range(LAG):
                    fc2(FC * end + f - LAG, FC + f - LAG)
                for half in range(2):
                    turn_back(end - 1, 1, half)

            feed_forward(0, 0)

            def mixer_tile(t, par, before, behind):
                pe.wait_ge(turned_out, 2 * t + (2 * NT + 2))
                wait(pe, b_ready, t)
                for k in range(KC):
                    last = nc.tensor.matmul(ps_ab, wab_sb[:, k, :], xn[:, par, k, :],
                                            start=k == 0, stop=k == KC - 1)
                last.then_inc(ab_done, 1)
                wait(pe, c_ready, t)
                for k in range(KC):
                    last = nc.tensor.matmul(ps_c, wc_sb[:, k, :], xn[:, par, k, :],
                                            start=k == 0, stop=k == KC - 1)
                last.then_inc(c_done, 1)
                wait(pe, mix_added, 2 * t - 2)
                for a in range(SUB):
                    for k in range(KC):
                        nc.tensor.matmul(ps_mix[:, par, a // 2, (a % 2) * D:(a % 2 + 1) * D],
                                         xn[:, par, k, a * P:(a + 1) * P], wd_sb[:, k, :],
                                         start=a % 2 == 0 and k == 0, stop=False, skip_group_check=True)
                if behind:
                    for c in range(KC):
                        turn(t + (NT + 1), c)
                pe.wait_ge(cs_ready, t + 1)
                for a in range(SUB):
                    mm = nc.tensor.matmul(ps_mix[:, par, a // 2, (a % 2) * D:(a % 2 + 1) * D],
                                          cs_sb[:, par, a * P:(a + 1) * P], wy_sb[:, :],
                                          start=False, stop=a % 2 == 1, skip_group_check=True)
                    if a % 2:
                        mm.then_inc(mix_done, 1)

            pe.wait_ge(mixer_ready, 1)
            for c in range(KC):
                turn(NT, c)
            pe.wait_ge(ffn_added, 2 * NT)
            over_tiles(pe, mixer_tile)

            pe.wait_ge(mix_added, 2 * NT)
            feed_forward(NT, 2 * NT)


_INS = ['L0_attn_x', 'L0_attn_Wa', 'L0_attn_ba', 'L0_attn_Wb', 'L0_attn_bb', 'L0_attn_Wc', 'L0_attn_bc',
        'L0_attn_Wd', 'L0_attn_bd', 'L0_attn_Wy', 'L0_attn_by', 'L0_ffn_ln_gamma', 'L0_ffn_ln_beta',
        'L0_ffn_fc1_q', 'L0_ffn_fc1_scales', 'L0_ffn_fc1_bias', 'L0_ffn_fc2_q', 'L0_ffn_fc2_scales',
        'L0_ffn_fc2_bias']


def kernel(**inputs):
    import numpy as _np
    import concourse.bacc as _bacc
    from concourse import mybir as _mybir
    from concourse.bass_utils import run_bass_kernel_spmd as _run

    nc = _bacc.Bacc("TRN2", target_bir_lowering=False, num_devices=1)
    arrays, args = {}, []
    for name in _INS:
        a = _np.ascontiguousarray(inputs[name])
        arrays[f"in_{name}"] = a
        args.append(nc.dram_tensor(f"in_{name}", a.shape, _mybir.dt.from_np(a.dtype), kind="ExternalInput").ap())
    shape = inputs['L0_attn_x'].shape
    out = nc.dram_tensor("out_x", shape, _mybir.dt.float32, kind="ExternalOutput").ap()
    macaron_kernel(nc, *args, out)
    r = _run(nc, [arrays], core_ids=[0])
    return r.results[0]["out_x"]
```

```python
from contextlib import ExitStack

import concourse.bass as bass
from concourse import mybir

ALU = mybir.AluOpType
ACT = mybir.ActivationFunctionType
AX = mybir.AxisListType
F32 = mybir.dt.float32
F32R = mybir.dt.float32r
I32 = mybir.dt.int32

P = 128
TILE = 512
SUB = TILE // P
LAG = 4
WIDE = 4096.0
EPS = 1e-5
ZERO_POINT = 128.0


def macaron_kernel(nc, x, wa, ba, wb, bb, wc, bc, wd, bd, wy, by, gamma, beta,
                   q1, s1, b1, q2, s2, b2, out):
    B, S, D = x.shape
    N = wa.shape[1]
    F = q1.shape[1]
    NT = B * S // TILE
    KC = D // P
    FC = F // P
    PAIRS = (NT - 4) // 2
    HALF = FC // 2
    SUMS = HALF + 1
    assert KC == 2 and 2 * N == P and S == 2 * TILE and FC == 8 and NT % 2 == 0
    assert s1.shape[0] == KC and s2.shape[0] == FC

    x_view = x.rearrange("b s d -> (b s) d").rearrange("(t a p) d -> p t a d", p=P, a=SUB)
    out_view = out.rearrange("b s d -> (b s) d").rearrange("(t a p) d -> p t a d", p=P, a=SUB)

    R_S1, R_B1 = 0, KC * FC
    R_S2 = R_B1 + FC
    R_B2 = R_S2 + FC * KC
    R_GAMMA = R_B2 + KC
    R_BETA = R_GAMMA + KC
    R_AB = R_BETA + KC
    R_C = R_AB + 1
    ROWS = R_C + 1

    with ExitStack() as ctx:
        def sb(name, shape, dt=F32):
            return ctx.enter_context(nc.sbuf_tensor(name, shape, dt))

        def sem(name):
            return ctx.enter_context(nc.semaphore(name))

        resid = sb("resid", [P, NT, SUB, D])
        q1_int = sb("q1_int", [P, KC, F], I32)
        q2_int = sb("q2_int", [P, FC, D], I32)
        q1_sb = sb("q1_sb", [P, KC, F], F32R)
        q1_low = sb("q1_low", [P, KC, F], F32R)
        q2_sb = sb("q2_sb", [P, HALF, KC, P], F32R)
        q2_low = sb("q2_low", [P, HALF, KC, P], F32R)
        w2_hi = sb("w2_hi", [P, HALF, KC, P], F32R)
        w2_lo = sb("w2_lo", [P, HALF, KC, P], F32R)
        largest = sb("largest", [P, 4])
        wide_flag = sb("wide_flag", [1, 1], I32)
        wab_sb = sb("wab_sb", [P, KC, 2 * N])
        wc_sb = sb("wc_sb", [P, KC, N])
        wd_sb = sb("wd_sb", [P, KC, D])
        wy_sb = sb("wy_sb", [N + 1, D])
        bias_rows = sb("bias_rows", [N + 1, 2, D])
        rows = sb("rows", [ROWS, P])
        cols = sb("cols", [P, ROWS])
        ident = sb("ident", [P, P])
        minus_half = sb("minus_half", [P, 2 * SUB])
        stats = sb("stats", [P, SUB, 6])
        mean_var = sb("mean_var", [P, SUB, 2])
        var_terms = sb("var_terms", [P, 2 * SUB])
        rstd = sb("rstd", [P, 2 * SUB])
        res_scale = sb("res_scale", [P, SUB])
        res_shift = sb("res_shift", [P, SUB])
        wait_holder = sb("wait_holder", [P, 1])
        xhat = sb("xhat", [P, SUB, D])
        h_full = sb("h_full", [P, KC, TILE])
        h_hi = sb("h_hi", [P, 2, KC, TILE], F32R)
        h_lo = sb("h_lo", [P, 2, KC, TILE], F32R)
        u_sb = sb("u_sb", [P, 2, TILE])
        y_sb = sb("y_sb", [P, 4, TILE])
        g_full = sb("g_full", [P, 2, TILE])
        g_hi = sb("g_hi", [P, 4, TILE], F32R)
        g_lo = sb("g_lo", [P, 4, TILE], F32R)
        z_acc = sb("z_acc", [P, 2, KC, TILE])
        assert HALF * D == KC * TILE
        s2_wide = z_acc[:, 0, :, :].rearrange("p k (j n d) -> p (k j) n d", n=KC, d=P)
        w2_full = z_acc[:, 1, :, :].rearrange("p k (j n d) -> p (k j) n d", n=KC, d=P)
        q2_groups = q2_int[:, :, :].rearrange("p g (n d) -> p g n d", n=KC)
        assert FC * D == 2 * KC * TILE
        xn = q2_int[:, :, :].bitcast(F32).rearrange("p g d -> p (g d)")\
            .rearrange("p (b k n) -> p b k n", b=2, k=KC)
        a_sb, b_sb, c_sb = u_sb[0:N, :, :], y_sb[0:N, 0:2, :], g_full[0:N, :, :]
        drive, state = h_full[0:N, :, :], z_acc[0:N, 0, :, :]
        cs_sb = sb("cs_sb", [N + 1, 2, TILE])

        ps_fc1 = ctx.enter_context(nc.psum_tensor("ps_fc1", [P, 2, KC, TILE], F32))
        ps_z = ctx.enter_context(nc.psum_tensor("ps_z", [P, KC, TILE], F32))
        ps_tr = ctx.enter_context(nc.psum_tensor("ps_tr", [P, TILE], F32))
        ps_back = ctx.enter_context(nc.psum_tensor("ps_back", [P, TILE], F32))
        ps_ab = ps_z[:, 0, :]
        ps_c = ps_z[0:N, 1, :]
        ps_mix = ps_fc1

        x_loaded = [sem("x_loaded_even"), sem("x_loaded_odd")]
        rows_zero = sem("rows_zero")
        rows_loaded = sem("rows_loaded")
        q1_loaded = sem("q1_loaded")
        q2_loaded = sem("q2_loaded")
        mixer_loaded = sem("mixer_loaded")
        ident_zero = sem("ident_zero")
        consts_ready = sem("consts_ready")
        rows_turned = sem("rows_turned")
        cols_ready = sem("cols_ready")
        q1_ready = sem("q1_ready")
        q2_ready = sem("q2_ready")
        s2_loaded = sem("s2_loaded")
        w2_int_ready = sem("w2_int_ready")
        w2_full_ready = sem("w2_full_ready")
        w2_hi_ready = sem("w2_hi_ready")
        w2_ready = sem("w2_ready")
        largest_found = sem("largest_found")
        largest_turned = sem("largest_turned")
        flag_ready = sem("flag_ready")
        wide_full = sem("wide_full")
        wide_ready = sem("wide_ready")
        mixer_ready = sem("mixer_ready")
        stored = sem("stored")
        stats_done = sem("stats_done")
        aggr_done = sem("aggr_done")
        var_ready = sem("var_ready")
        rstd_ready = sem("rstd_ready")
        res_terms = sem("res_terms")
        xhat_ready = sem("xhat_ready")
        resid_scaled = sem("resid_scaled")
        turned = sem("turned")
        turned_out = sem("turned_out")
        h_ready = sem("h_ready")
        fc1_done = sem("fc1_done")
        u_ready = sem("u_ready")
        y_ready = sem("y_ready")
        g_hi_ready = sem("g_hi_ready")
        g_ready = sem("g_ready")
        fc2_done = sem("fc2_done")
        z_added = [sem(f"z{n}_added") for n in range(KC)]
        back_done = sem("back_done")
        ffn_added = sem("ffn_added")
        ab_done = sem("ab_done")
        c_done = sem("c_done")
        a_ready = sem("a_ready")
        b_ready = sem("b_ready")
        c_ready = sem("c_ready")
        drive_ready = sem("drive_ready")
        state_ready = sem("state_ready")
        cs_ready = sem("cs_ready")
        mix_done = sem("mix_done")
        mix_added = sem("mix_added")

        def col(r):
            return cols[:, r:r + 1]

        def wait(eng, signal, count):
            if type(count) is not int or count > 0:
                eng.wait_ge(signal, count)

        def in_sum(g, n):
            return g // HALF == n

        def added_before(g, n):
            return (0 if g < HALF else g - HALF + 1) if n == 0 else min(g, HALF)

        def over_tiles(eng, tile):
            tile(0, 0, 0, 2)
            tile(1, 1, 1, 2)
            with eng.Fori(0, PAIRS) as i:
                tile(2 * i + 2, 0, 2, 2)
                tile(2 * i + 3, 1, 2, 2)
            tile(NT - 2, 0, 2, 1)
            tile(NT - 1, 1, 2, 0)

        block = ctx.enter_context(nc.Block())

        @block.sync
        def _(sp):
            sp.wait_ge(rows_zero, 1)
            small = [(s1.rearrange("k (c p) -> (k c) p", p=P), R_S1, KC * FC),
                     (b1.rearrange("(c p) -> c p", p=P), R_B1, FC),
                     (s2.rearrange("g (n p) -> (g n) p", p=P), R_S2, FC * KC),
                     (b2.rearrange("(n p) -> n p", p=P), R_B2, KC),
                     (gamma.rearrange("(k p) -> k p", p=P), R_GAMMA, KC),
                     (beta.rearrange("(k p) -> k p", p=P), R_BETA, KC)]
            sp.dma_start(resid[:, 0, :, :], x_view[:, 0, :, :]).then_inc(x_loaded[0], 16)
            for src, r, n in small:
                sp.dma_start(rows[r:r + n, :], src).then_inc(rows_loaded, 16)
            for v, r, at in ((ba, R_AB, 0), (bb, R_AB, N), (bc, R_C, 0)):
                sp.dma_start(rows[r:r + 1, at:at + N], v.rearrange("(a n) -> a n", a=1)).then_inc(rows_loaded, 16)
            for n in range(KC):
                scales = s2[n * HALF:(n + 1) * HALF, n * P:(n + 1) * P].rearrange("(o j) d -> o j d", o=1)
                sp.dma_start(s2_wide[:, :, n, :], scales.broadcast_to([P, HALF, P])).then_inc(s2_loaded, 16)
            sp.dma_start(resid[:, 1, :, :], x_view[:, 1, :, :]).then_inc(x_loaded[1], 16)
            with sp.Fori(0, NT // 2 - 1) as i:
                for par in range(2):
                    sp.wait_ge(x_loaded[par], 16 * i + 16)
                    sp.dma_start(resid[:, 2 * i + (2 + par), :, :],
                                 x_view[:, 2 * i + (2 + par), :, :]).then_inc(x_loaded[par], 16)

            with sp.Fori(0, NT) as t:
                sp.wait_ge(ffn_added, 2 * t + (2 * NT + 2))
                sp.dma_start(out_view[:, t, :, :], resid[:, t, :, :]).then_inc(stored, 16)
            sp.wait_ge(stored, 16 * NT)

        @block.gpsimd
        def _(pool):
            nc.gpsimd.memset(rows[:, :], 0.0).then_inc(rows_zero, 1)
            nc.gpsimd.memset(ident[:, :], 0.0).then_inc(ident_zero, 1)
            pool.wait_ge(ident_zero, 1)
            nc.gpsimd.affine_select(out=ident[:, :], in_=ident[:, :], compare_op=ALU.not_equal, fill=1.0,
                                    base=0, pattern=[[-1, P]], channel_multiplier=1).then_inc(consts_ready, 1)
            pool.wait_ge(consts_ready, 1)
            nc.gpsimd.memset(cs_sb[N:N + 1, :, :], 1.0).then_inc(consts_ready, 1)
            pool.wait_ge(consts_ready, 2)
            nc.gpsimd.memset(minus_half[:, :], -0.5).then_inc(consts_ready, 1)
            pool.wait_ge(consts_ready, 3)

            def rsqrt(ln, n):
                pool.wait_ge(var_ready, ln + 1)
                nc.gpsimd.tensor_tensor(rstd[:, 0:n], var_terms[:, 0:n], minus_half[:, 0:n],
                                        ALU.pow).then_inc(rstd_ready, 1)

            def h_low(ln, ff, par, c):
                pool.wait_ge(turned_out, 2 * ln + (c + 1))
                wait(pool, fc1_done, FC * ff - FC)
                nc.gpsimd.tensor_tensor(h_lo[:, par, c, :], h_full[:, c, :], h_hi[:, par, c, :].bitcast(F32),
                                        ALU.subtract).then_inc(h_ready, 1)

            def g_low(step, slot):
                pool.wait_ge(g_hi_ready, step + 1)
                wait(pool, fc2_done, 2 * step - 6)
                nc.gpsimd.tensor_tensor(g_lo[:, slot % 4, :], g_full[:, slot % 2, :],
                                        g_hi[:, slot % 4, :].bitcast(F32), ALU.subtract).then_inc(g_ready, 1)

            def feed_forward(ff0, ln0):
                def tile(t, par, before, behind):
                    ff, ln = t + ff0, t + ln0
                    for f in range(FC):
                        if before or f >= 1:
                            g_low(FC * ff + (f - 1), f + 7)
                        if behind >= 1 and f in (3, 5):
                            h_low(ln + 1, ff + 1, 1 - par, f // 5)
                        if behind >= 2 and f == 2:
                            rsqrt(ln + 2, 2 * SUB)
                rsqrt(ln0, 2 * SUB)
                if ff0 == 0:
                    pool.wait_ge(s2_loaded, 16 * KC)
                    pool.wait_ge(w2_int_ready, KC)
                    nc.gpsimd.tensor_tensor(w2_full, w2_full, s2_wide, ALU.mult).then_inc(w2_full_ready, 1)
                for c in range(KC):
                    h_low(ln0, ff0, 0, c)
                if ff0 == 0:
                    pool.wait_ge(w2_hi_ready, 1)
                    nc.gpsimd.tensor_tensor(w2_lo[:, :, :, :], w2_full, w2_hi[:, :, :, :].bitcast(F32),
                                            ALU.subtract).then_inc(w2_ready, 1)
                rsqrt(ln0 + 1, 2 * SUB)
                over_tiles(pool, tile)
                g_low(FC * (ff0 + NT) - 1, 7)

            feed_forward(0, 0)

            def mixer_tile(t, par, before, behind):
                if behind:
                    rsqrt(t + (NT + 1), SUB)
            rsqrt(NT, SUB)
            over_tiles(pool, mixer_tile)

            feed_forward(NT, 2 * NT)

        @block.scalar
        def _(act):
            act.dma_start(q1_int[:, :, :], q1.rearrange("(k p) f -> p k f", p=P)).then_inc(q1_loaded, 16)
            act.dma_start(q2_int[:, :, :], q2.rearrange("(g p) d -> p g d", p=P)).then_inc(q2_loaded, 16)
            for dst, src in ((wab_sb[:, :, 0:N], wa), (wab_sb[:, :, N:2 * N], wb), (wc_sb[:, :, :], wc),
                             (wd_sb[:, :, :], wd)):
                act.dma_start(dst, src.rearrange("(k p) n -> p k n", p=P)).then_inc(mixer_loaded, 16)
            act.dma_start(wy_sb[0:N, :], wy).then_inc(mixer_loaded, 16)
            for i, v in enumerate((by, bd)):
                act.dma_start(bias_rows[N:N + 1, i, :], v.rearrange("(a n) -> a n", a=1)).then_inc(mixer_loaded, 16)
            act.wait_ge(q1_loaded, 16)
            nc.scalar.activation(q1_sb[:, :, :], q1_int[:, :, :], ACT.Copy, bias=-ZERO_POINT).then_inc(q1_ready, 1)
            act.wait_ge(q2_loaded, 16)
            for n in range(KC):
                nc.scalar.activation(q2_sb[:, :, n, :], q2_groups[:, (1 - n) * HALF:(2 - n) * HALF, n, :],
                                     ACT.Copy, bias=-ZERO_POINT).then_inc(q2_ready, 1)
                nc.scalar.activation(w2_full[:, :, n, :], q2_groups[:, n * HALF:(n + 1) * HALF, n, :],
                                     ACT.Copy, bias=-ZERO_POINT).then_inc(w2_int_ready, 1)
            act.wait_ge(rows_turned, 1)
            nc.scalar.activation(cols[:, :], ps_back[:, 0:ROWS], ACT.Copy).then_inc(cols_ready, 1)
            act.wait_ge(cols_ready, 1)

            def affine(ln, ff, par, c, outs=(0, 1)):
                if 0 in outs:
                    act.wait_ge(turned, 2 * ln + (c + 1))
                    wait(act, h_ready, 2 * ff + (c - 1))
                    nc.scalar.activation(h_full[:, c, :], ps_tr[:, :], ACT.Identity, bias=col(R_BETA + c),
                                         scale=col(R_GAMMA + c))
                if 1 in outs:
                    wait(act, fc1_done, FC * ff - FC)
                    nc.scalar.activation(h_hi[:, par, c, :], ps_tr[:, :], ACT.Identity, bias=col(R_BETA + c),
                                         scale=col(R_GAMMA + c)).then_inc(turned_out, 1)

            def first_group(step, f):
                act.wait_ge(fc1_done, step + 1)
                wait(act, y_ready, step - 1)
                nc.scalar.activation(u_sb[:, f % 2, :], ps_fc1[:, f % 2, 0, :], ACT.Identity,
                                     bias=col(R_B1 + f), scale=col(R_S1 + f)).then_inc(u_ready, 1)

            def silu(step, slot):
                act.wait_ge(y_ready, step + 1)
                wait(act, g_ready, step - 1)
                nc.scalar.activation(g_full[:, slot % 2, :], y_sb[:, slot % 4, :], ACT.Silu)
                wait(act, fc2_done, 2 * step - 6)
                nc.scalar.activation(g_hi[:, slot % 4, :], y_sb[:, slot % 4, :],
                                     ACT.Silu).then_inc(g_hi_ready, 1)

            def feed_forward(ff0, ln0):
                def tile(t, par, before, behind):
                    ff, ln = t + ff0, t + ln0
                    for f in range(FC):
                        first_group(FC * ff + f, f)
                        if before or f >= 1:
                            silu(FC * ff + (f - 1), f + 7)
                        if behind and f in (0, 1, 3, 4):
                            affine(ln + 1, ff + 1, 1 - par, f // 3, (f % 3,))
                for c in range(KC):
                    affine(ln0, ff0, 0, c)
                over_tiles(act, tile)
                silu(FC * (ff0 + NT) - 1, 7)

            feed_forward(0, 0)

            def turn_out(t, par, c):
                act.wait_ge(turned, 2 * t + (2 * NT + c + 1))
                wait(act, mix_done, 2 * t - 2)
                nc.scalar.activation(xn[:, par, c, :], ps_tr[:, :], ACT.Copy).then_inc(turned_out, 1)

            def mixer_tile(t, par, before, behind):
                act.wait_ge(ab_done, t + 1)
                wait(act, cs_ready, t)
                nc.scalar.activation(a_sb[:, par, :], ps_ab[0:N, :], ACT.Sigmoid,
                                     bias=cols[0:N, R_AB:R_AB + 1]).then_inc(a_ready, 1)
                nc.scalar.activation(b_sb[:, par, :], ps_ab[N:2 * N, :], ACT.Identity,
                                     bias=cols[N:2 * N, R_AB:R_AB + 1]).then_inc(b_ready, 1)
                act.wait_ge(c_done, t + 1)
                nc.scalar.activation(c_sb[:, par, :], ps_c, ACT.Tanh,
                                     bias=cols[0:N, R_C:R_C + 1]).then_inc(c_ready, 1)
                if behind:
                    for c in range(KC):
                        turn_out(t + 1, 1 - par, c)
            for c in range(KC):
                turn_out(0, 0, c)
            over_tiles(act, mixer_tile)

            feed_forward(NT, 2 * NT)

        @block.vector
        def _(dve):
            def statistics(t, blocks=range(SUB)):
                for a in blocks:
                    last = nc.vector.bn_stats(stats[:, a, :], resid[:, t, a, :])
                if blocks[-1] == SUB - 1:
                    last.then_inc(stats_done, 1)

            def variance(ln, twice):
                dve.wait_ge(stats_done, ln + 1)
                nc.vector.memset(wait_holder[:, :], 0.0)
                for a in range(SUB):
                    last = nc.vector.bn_aggr(mean_var[:, a, :], stats[:, a, :])
                last.then_inc(aggr_done, 1)
                dve.wait_ge(aggr_done, ln + 1)
                last = nc.vector.tensor_scalar(var_terms[:, 0:SUB], mean_var[:, :, 1], EPS, None, ALU.add)
                if twice:
                    last = nc.vector.tensor_scalar(var_terms[:, SUB:2 * SUB], mean_var[:, :, 1], 1.0 + EPS,
                                                   EPS * EPS, ALU.mult, ALU.add)
                last.then_inc(var_ready, 1)

            def normalise(ln, t, twice, blocks=range(SUB)):
                if blocks[0] == 0:
                    dve.wait_ge(rstd_ready, ln + 1)
                    wait(dve, turned, 2 * ln)
                at = SUB if twice else 0
                for a in blocks:
                    last = nc.vector.tensor_scalar(xhat[:, a, :], resid[:, t, a, :], mean_var[:, a, 0:1],
                                                   rstd[:, at + a:at + a + 1], ALU.subtract, ALU.mult)
                if blocks[-1] == SUB - 1:
                    last.then_inc(xhat_ready, 1)

            def residual(ff, t, blocks=range(SUB)):
                if blocks[0] == 0:
                    nc.vector.tensor_scalar(res_scale[:, :], rstd[:, 0:SUB], 0.5, 1.0, ALU.mult, ALU.add)
                    nc.vector.scalar_tensor_tensor(out=res_shift[:, :], in0=mean_var[:, :, 0], scalar=-0.5,
                                                   in1=rstd[:, 0:SUB], op0=ALU.mult,
                                                   op1=ALU.mult).then_inc(res_terms, 1)
                    dve.wait_ge(res_terms, ff + 1)
                for a in blocks:
                    last = nc.vector.tensor_scalar(resid[:, t, a, :], resid[:, t, a, :], res_scale[:, a:a + 1],
                                                   res_shift[:, a:a + 1], ALU.mult, ALU.add)
                if blocks[-1] == SUB - 1:
                    last.then_inc(resid_scaled, 1)

            def second_group(step, f):
                dve.wait_ge(u_ready, step + 1)
                wait(dve, g_hi_ready, step - 3)
                nc.vector.scalar_tensor_tensor(out=y_sb[:, f % 4, :], in0=ps_fc1[:, f % 2, 1, :],
                                               scalar=col(R_S1 + FC + f), in1=u_sb[:, f % 2, :],
                                               op0=ALU.mult, op1=ALU.add).then_inc(y_ready, 1)

            def add_group(step, ff, g, par):
                for n in range(KC):
                    if in_sum(g, n) and g % HALF != HALF - 1:
                        continue
                    dve.wait_ge(fc2_done, 2 * step + (n + 1))
                    z, bank, scale = z_acc[:, par, n, :], ps_z[:, n, :], col(R_S2 + KC * g + n)
                    if added_before(g, n) == 0:
                        wait(dve, back_done, 2 * ff - 2)
                    else:
                        dve.wait_ge(z_added[n], SUMS * ff + added_before(g, n))
                    if in_sum(g, n) and n == 0:
                        op = nc.vector.tensor_scalar(z, bank, col(R_B2 + n), None, ALU.add)
                    elif in_sum(g, n):
                        op = nc.vector.tensor_tensor(z, bank, z, ALU.add)
                    elif g == 0:
                        op = nc.vector.tensor_scalar(z, bank, scale, col(R_B2 + n), ALU.mult, ALU.add)
                    else:
                        op = nc.vector.scalar_tensor_tensor(out=z, in0=bank, scalar=scale, in1=z,
                                                            op0=ALU.mult, op1=ALU.add)
                    op.then_inc(z_added[n], 1)

            def add_ffn(ff, t, half):
                dve.wait_ge(back_done, 2 * ff + (half + 1))
                dve.wait_ge(resid_scaled, ff + 1)
                part = resid[:, t, 2 * half:2 * half + 2, :]
                nc.vector.scalar_tensor_tensor(out=part, in0=ps_back[:, :].rearrange("p (a d) -> p a d", a=2),
                                               scalar=0.25, in1=part, op0=ALU.mult,
                                               op1=ALU.add).then_inc(ffn_added, 1)

            def feed_forward(ff0, ln0):
                def tile(t, par, before, behind):
                    ff, ln = t + ff0, t + ln0
                    for f in range(FC):
                        second_group(FC * ff + f, f)
                        if before or f >= LAG:
                            g = (f - LAG) % FC
                            if f >= LAG:
                                add_group(FC * ff + (f - LAG), ff, g, par)
                            else:
                                add_group(FC * ff + (f - LAG), ff - 1, g, 1 - par)
                        if behind >= 1 and f == 0:
                            residual(ff + 1, t + 1, range(2, SUB))
                        if behind >= 2:
                            if f == 1 and ff0 == 0:
                                dve.wait_ge(x_loaded[par], 8 * t + (32 if par == 0 else 24))
                            if f in (1, 2):
                                statistics(t + 2, range(2 * f - 2, 2 * f))
                            if f == 2:
                                variance(ln + 2, True)
                            if f in (4, 5):
                                normalise(ln + 2, t + 2, True, range(2 * f - 8, 2 * f - 6))
                            if f == 6:
                                residual(ff + 2, t + 2, range(2))
                        if before and f in (5, 7):
                            add_ffn(ff - 1, t - 1, (f - 5) // 2)

                if ff0 == 0:
                    dve.wait_ge(x_loaded[0], 16)
                statistics(0)
                variance(ln0, True)
                normalise(ln0, 0, True)
                residual(ff0, 0)
                if ff0 == 0:
                    prepare_weights()
                    dve.wait_ge(x_loaded[1], 16)
                statistics(1)
                variance(ln0 + 1, True)
                normalise(ln0 + 1, 1, True)
                residual(ff0 + 1, 1, range(2))
                over_tiles(dve, tile)
                end = ff0 + NT
                for f in range(LAG):
                    add_group(FC * end + f - LAG, end - 1, FC + f - LAG, 1)
                for half in range(2):
                    add_ffn(end - 1, NT - 1, half)

            def prepare_weights():
                dve.wait_ge(q1_ready, 1)
                nc.vector.tensor_reduce(out=largest[:, 0:1], in_=q1_sb[:, :, :].bitcast(F32), axis=AX.XY,
                                        op=ALU.max, apply_absolute_value=True)
                dve.wait_ge(q2_ready, KC)
                nc.vector.tensor_reduce(out=largest[:, 1:2], in_=q2_sb[:, :, :, :].bitcast(F32), axis=AX.XYZ,
                                        op=ALU.max, apply_absolute_value=True).then_inc(largest_found, 1)
                dve.wait_ge(largest_found, 1)
                nc.vector.tensor_reduce(out=largest[:, 2:3], in_=largest[:, 0:2], axis=AX.X,
                                        op=ALU.max).then_inc(largest_found, 1)
                dve.wait_ge(largest_turned, 1)
                nc.vector.tensor_reduce(out=largest[0:1, 3:4], in_=ps_z[0:1, 0, 0:P], axis=AX.X,
                                        op=ALU.max).then_inc(largest_found, 1)
                dve.wait_ge(largest_found, 3)
                nc.vector.tensor_scalar(wide_flag[:, :], largest[0:1, 3:4], WIDE, None,
                                        ALU.is_ge).then_inc(flag_ready, 1)
                dve.wait_ge(w2_full_ready, 1)
                nc.vector.tensor_copy(w2_hi[:, :, :, :], w2_full).then_inc(w2_hi_ready, 1)
                dve.wait_ge(mixer_loaded, 16 * 7)
                nc.vector.tensor_tensor(wy_sb[N:N + 1, :], bias_rows[N:N + 1, 0, :], bias_rows[N:N + 1, 1, :],
                                        ALU.add).then_inc(mixer_ready, 1)
                dve.wait_ge(cols_ready, 1)
                dve.wait_ge(flag_ready, 1)
                wide = dve.value_load(wide_flag[0:1, 0:1], min_val=0, max_val=1)
                with dve.If(wide > 0):
                    chunks = [(q1_low[:, k, :], q1_sb[:, k, :], q1_int[:, k, :]) for k in range(KC)]
                    chunks += [(q2_low[:, :, n, :], q2_sb[:, :, n, :],
                                q2_groups[:, (1 - n) * HALF:(2 - n) * HALF, n, :]) for n in range(KC)]
                    for i, (low, high, whole) in enumerate(chunks):
                        nc.vector.tensor_scalar(whole.bitcast(F32), whole, -ZERO_POINT, None,
                                                ALU.add).then_inc(wide_full, 1)
                        dve.wait_ge(wide_full, i + 1)
                        nc.vector.tensor_tensor(low, whole.bitcast(F32), high.bitcast(F32),
                                                ALU.subtract).then_inc(wide_ready, 1)

            feed_forward(0, 0)

            def scan(t, par):
                dve.wait_ge(b_ready, t + 1)
                nc.vector.scalar_tensor_tensor(out=drive[:, par, :], in0=a_sb[:, par, :], scalar=1.0,
                                               in1=b_sb[:, par, :], op0=ALU.subtract,
                                               op1=ALU.mult).then_inc(drive_ready, 1)
                dve.wait_ge(drive_ready, t + 1)
                nc.vector.tensor_tensor_scan(state[:, par, :], a_sb[:, par, :], drive[:, par, :],
                                             state[:, 0, TILE - 1:TILE] if par else 0.0,
                                             ALU.mult, ALU.subtract).then_inc(state_ready, 1)
                dve.wait_ge(state_ready, t + 1)
                dve.wait_ge(c_ready, t + 1)
                wait(dve, mix_done, 2 * t - 2)
                nc.vector.tensor_tensor(cs_sb[0:N, par, :], c_sb[:, par, :], state[:, par, :],
                                        ALU.mult).then_inc(cs_ready, 1)

            def add_mixer(t, par, half):
                dve.wait_ge(mix_done, 2 * t + (half + 1))
                part = resid[:, t, 2 * half:2 * half + 2, :]
                nc.vector.tensor_tensor(part, ps_mix[:, par, half, :].rearrange("p (a d) -> p a d", a=2), part,
                                        ALU.add).then_inc(mix_added, 1)

            def mixer_tile(t, par, before, behind):
                if behind:
                    statistics(t + 1)
                    variance(t + (NT + 1), False)
                    normalise(t + (NT + 1), t + 1, False)
                scan(t, par)
                for half in range(2):
                    add_mixer(t, par, half)

            statistics(0)
            variance(NT, False)
            normalise(NT, 0, False)
            over_tiles(dve, mixer_tile)

            dve.wait_ge(mix_added, 2 * NT)
            feed_forward(NT, 2 * NT)

        @block.tensor
        def _(pe):
            pe.wait_ge(consts_ready, 3)
            pe.wait_ge(rows_loaded, 16 * 9)
            nc.tensor.transpose(ps_back[:, 0:ROWS], rows[:, :], ident[0:ROWS, 0:ROWS]).then_inc(rows_turned, 1)

            def turn(ln, c):
                pe.wait_ge(xhat_ready, ln + 1)
                wait(pe, turned_out, 2 * ln + c)
                for a in range(SUB):
                    last = nc.tensor.transpose(ps_tr[:, a * P:(a + 1) * P], xhat[:, a, c * P:(c + 1) * P],
                                               ident[:, :])
                last.then_inc(turned, 1)

            def products(out, pairs, start=True, stop=True):
                for i, (w, v) in enumerate(pairs):
                    last = nc.tensor.matmul(out, w, v, start=start and i == 0, stop=stop and i == len(pairs) - 1)
                return last

            def fc1(step, ff, f, par):
                if f == 0:
                    pe.wait_ge(h_ready, 2 * ff + 2)
                wait(pe, y_ready, step - 1)
                for k in range(KC):
                    last = products(ps_fc1[:, f % 2, k, :],
                                    [(w[:, k, f * P:(f + 1) * P], h[:, par, k, :])
                                     for w in q1_parts for h in (h_hi, h_lo)])
                last.then_inc(fc1_done, 1)

            def fc2(step, ff, g):
                pe.wait_ge(g_ready, step + 1)
                for n in range(KC):
                    first = not in_sum(g, n) or g % HALF == 0
                    if first:
                        wait(pe, z_added[n], SUMS * ff + added_before(g, n))
                    parts = (w2_hi, w2_lo) if in_sum(g, n) else q2_parts
                    products(ps_z[:, n, :], [(w[:, g % HALF, n, :], v[:, g % 4, :])
                                             for w in parts for v in (g_hi, g_lo)],
                             start=first, stop=not in_sum(g, n) or g % HALF == HALF - 1).then_inc(fc2_done, 1)

            def turn_back(ff, par, half):
                for n in range(KC):
                    pe.wait_ge(z_added[n], SUMS * ff + SUMS)
                wait(pe, ffn_added, 2 * ff + half)
                for a in range(2):
                    at = (2 * half + a) * P
                    for n in range(KC):
                        last = nc.tensor.transpose(ps_back[:, a * D + n * P:a * D + (n + 1) * P],
                                                   z_acc[:, par, n, at:at + P], ident[:, :])
                last.then_inc(back_done, 1)

            def feed_forward(ff0, ln0):
                def tile(t, par, before, behind):
                    ff, ln = t + ff0, t + ln0
                    for f in range(FC):
                        fc1(FC * ff + f, ff, f, par)
                        if before or f >= LAG:
                            fc2(FC * ff + (f - LAG), ff if f >= LAG else ff - 1, (f - LAG) % FC)
                        if behind and f in (0, 3):
                            turn(ln + 1, f // 3)
                        if before and f in (4, 6):
                            turn_back(ff - 1, 1 - par, (f - 4) // 2)
                if ff0:
                    for c in range(KC):
                        turn(ln0, c)
                over_tiles(pe, tile)
                end = ff0 + NT
                for f in range(LAG):
                    fc2(FC * end + f - LAG, end - 1, FC + f - LAG)
                for half in range(2):
                    turn_back(end - 1, 1, half)

            def mixer_tile(t, par, before, behind):
                pe.wait_ge(turned_out, 2 * t + (2 * NT + 2))
                wait(pe, b_ready, t)
                for k in range(KC):
                    last = nc.tensor.matmul(ps_ab, wab_sb[:, k, :], xn[:, par, k, :],
                                            start=k == 0, stop=k == KC - 1)
                last.then_inc(ab_done, 1)
                wait(pe, c_ready, t)
                for k in range(KC):
                    last = nc.tensor.matmul(ps_c, wc_sb[:, k, :], xn[:, par, k, :],
                                            start=k == 0, stop=k == KC - 1)
                last.then_inc(c_done, 1)
                wait(pe, mix_added, 2 * t - 2)
                for a in range(SUB):
                    for k in range(KC):
                        nc.tensor.matmul(ps_mix[:, par, a // 2, (a % 2) * D:(a % 2 + 1) * D],
                                         xn[:, par, k, a * P:(a + 1) * P], wd_sb[:, k, :],
                                         start=a % 2 == 0 and k == 0, stop=False, skip_group_check=True)
                if behind:
                    for c in range(KC):
                        turn(t + (NT + 1), c)
                pe.wait_ge(cs_ready, t + 1)
                for a in range(SUB):
                    mm = nc.tensor.matmul(ps_mix[:, par, a // 2, (a % 2) * D:(a % 2 + 1) * D],
                                          cs_sb[:, par, a * P:(a + 1) * P], wy_sb[:, :],
                                          start=False, stop=a % 2 == 1, skip_group_check=True)
                    if a % 2:
                        mm.then_inc(mix_done, 1)

            def program():
                feed_forward(0, 0)

                pe.wait_ge(mixer_ready, 1)
                for c in range(KC):
                    turn(NT, c)
                pe.wait_ge(ffn_added, 2 * NT)
                over_tiles(pe, mixer_tile)

                pe.wait_ge(mix_added, 2 * NT)
                feed_forward(NT, 2 * NT)

            for c in range(KC):
                turn(0, c)
            pe.wait_ge(largest_found, 2)
            nc.tensor.transpose(ps_z[0:1, 0, 0:P], largest[:, 2:3], ident[:, :]).then_inc(largest_turned, 1)
            pe.wait_ge(cols_ready, 1)
            pe.wait_ge(w2_ready, 1)
            pe.wait_ge(flag_ready, 1)
            wide = pe.value_load(wide_flag[0:1, 0:1], min_val=0, max_val=1)
            with pe.If(wide > 0):
                q1_parts, q2_parts = (q1_sb, q1_low), (q2_sb, q2_low)
                pe.wait_ge(wide_ready, 2 * KC)
                program()
            with pe.Else():
                q1_parts, q2_parts = (q1_sb,), (q2_sb,)
                program()


_INS = ['L0_attn_x', 'L0_attn_Wa', 'L0_attn_ba', 'L0_attn_Wb', 'L0_attn_bb', 'L0_attn_Wc', 'L0_attn_bc',
        'L0_attn_Wd', 'L0_attn_bd', 'L0_attn_Wy', 'L0_attn_by', 'L0_ffn_ln_gamma', 'L0_ffn_ln_beta',
        'L0_ffn_fc1_q', 'L0_ffn_fc1_scales', 'L0_ffn_fc1_bias', 'L0_ffn_fc2_q', 'L0_ffn_fc2_scales',
        'L0_ffn_fc2_bias']


def kernel(**inputs):
    import numpy as _np
    import concourse.bacc as _bacc
    from concourse import mybir as _mybir
    from concourse.bass_utils import run_bass_kernel_spmd as _run

    nc = _bacc.Bacc("TRN2", target_bir_lowering=False, num_devices=1)
    arrays, args = {}, []
    for name in _INS:
        a = _np.ascontiguousarray(inputs[name])
        arrays[f"in_{name}"] = a
        args.append(nc.dram_tensor(f"in_{name}", a.shape, _mybir.dt.from_np(a.dtype), kind="ExternalInput").ap())
    shape = inputs['L0_attn_x'].shape
    out = nc.dram_tensor("out_x", shape, _mybir.dt.float32, kind="ExternalOutput").ap()
    macaron_kernel(nc, *args, out)
    r = _run(nc, [arrays], core_ids=[0])
    return r.results[0]["out_x"]
```

```python
from contextlib import ExitStack

import concourse.bass as bass
from concourse import mybir

ALU = mybir.AluOpType
ACT = mybir.ActivationFunctionType
AX = mybir.AxisListType
F32 = mybir.dt.float32
F32R = mybir.dt.float32r
I32 = mybir.dt.int32

P = 128
TILE = 512
SUB = TILE // P
LAG = 4
WIDE = 4096.0
EPS = 1e-5
ZERO_POINT = 128.0


def macaron_kernel(nc, x, wa, ba, wb, bb, wc, bc, wd, bd, wy, by, gamma, beta,
                   q1, s1, b1, q2, s2, b2, out):
    B, S, D = x.shape
    N = wa.shape[1]
    F = q1.shape[1]
    NT = B * S // TILE
    KC = D // P
    FC = F // P
    PAIRS = (NT - 4) // 2
    SCALED = (4, 3)
    scaled_groups = (range(0, SCALED[0]), range(FC - SCALED[1], FC))
    whole_groups = (range(SCALED[0], FC), range(0, FC - SCALED[1]))
    SUMS = tuple(len(whole) + 1 for whole in whole_groups)
    FIRST = (1, 0, 1, 1, 0, 0, 1, 0)
    BANKS = (((1, 1, 1, 1, 2, 1, 1, 0), (0, 0, 2, 0, 0, 2, 2, 2)),
             ((0, 0, 0, 0, 2, 0, 0, 1), (1, 1, 2, 1, 1, 2, 2, 2)))
    STATISTICS_AT = (1, 2)
    VARIANCE_AT = 2
    RSQRT_AT = 2
    NORMALISE_AT = ((4, 5), (6, 7))
    RESIDUAL_AT = (6, 7)
    TURN_AT = ((1, 3), (2, 4))
    TURN_OUT_AT = ((1, 2, 3, 4), (2, 3, 4, 5))
    LOWER_PART_AT = ((3, 4), (3, 5))
    TURN_BACK_AT = (5, 7)
    ADD_AT = (5, 7)
    assert KC == 2 and 2 * N == P and S == 2 * TILE and FC == 8 and NT % 2 == 0
    assert s1.shape[0] == KC and s2.shape[0] == FC

    x_view = x.rearrange("b s d -> (b s) d").rearrange("(t a p) d -> p t a d", p=P, a=SUB)
    out_view = out.rearrange("b s d -> (b s) d").rearrange("(t a p) d -> p t a d", p=P, a=SUB)

    R_S1, R_B1 = 0, KC * FC
    R_S2 = R_B1 + FC
    R_B2 = R_S2 + FC * KC
    R_GAMMA = R_B2 + KC
    R_BETA = R_GAMMA + KC
    R_AB = R_BETA + KC
    R_C = R_AB + 1
    ROWS = R_C + 1

    with ExitStack() as ctx:
        def sb(name, shape, dt=F32):
            return ctx.enter_context(nc.sbuf_tensor(name, shape, dt))

        def sem(name):
            return ctx.enter_context(nc.semaphore(name))

        resid = sb("resid", [P, NT, SUB, D])
        q1_int = sb("q1_int", [P, KC, F], I32)
        q2_int = sb("q2_int", [P, FC, D], I32)
        q1_sb = sb("q1_sb", [P, KC, F], F32R)
        q1_low = sb("q1_low", [P, KC, F], F32R)
        whole_place = (slice(0, FC - SCALED[0]), slice(FC - SCALED[0], KC * FC - sum(SCALED)))
        scaled_place = (slice(0, SCALED[0]), slice(SCALED[0], sum(SCALED)))
        q2_sb = sb("q2_sb", [P, KC * FC - sum(SCALED), P], F32R)
        q2_low = sb("q2_low", [P, KC * FC - sum(SCALED), P], F32R)
        w2_hi = sb("w2_hi", [P, sum(SCALED), P], F32R)
        w2_lo = sb("w2_lo", [P, sum(SCALED), P], F32R)
        largest = sb("largest", [P, 4])
        wide_flag = sb("wide_flag", [1, 1], I32)
        wab_sb = sb("wab_sb", [P, KC, 2 * N])
        wd_sb = sb("wd_sb", [P, KC, D])
        wc_parts = sb("wc_parts", [P, KC, 2, N], F32R)
        wy_hi = sb("wy_hi", [P, D], F32R)
        wy_lo = sb("wy_lo", [P, D], F32R)
        bias_parts = sb("bias_parts", [N, 2, D], F32R)
        ones = sb("ones", [N, P], F32R)
        rows = sb("rows", [ROWS, P])
        cols = sb("cols", [P, ROWS])
        ident = sb("ident", [P, P])
        minus_half = sb("minus_half", [P, 2 * SUB])
        stats = sb("stats", [P, SUB, 6])
        mean_var = sb("mean_var", [P, SUB, 2])
        var_terms = sb("var_terms", [P, 2 * SUB])
        rstd = sb("rstd", [P, 2 * SUB])
        res_scale = sb("res_scale", [P, SUB])
        res_shift = sb("res_shift", [P, SUB])
        wait_holder = sb("wait_holder", [P, 1])
        silu_table = sb("silu_table", [P, 1])
        xhat = sb("xhat", [P, SUB, D])
        h_full = sb("h_full", [P, KC, TILE])
        h_hi = sb("h_hi", [P, 2, KC, TILE], F32R)
        h_lo = sb("h_lo", [P, 2, KC, TILE], F32R)
        u_sb = sb("u_sb", [P, 2, TILE])
        y_sb = sb("y_sb", [P, 4, TILE])
        g_full = sb("g_full", [P, 2, TILE])
        g_hi = sb("g_hi", [P, 4, TILE], F32R)
        g_lo = sb("g_lo", [P, 4, TILE], F32R)
        z_acc = sb("z_acc", [P, 2, KC, TILE])
        s2_wide, w2_full = (z_acc[:, b, :, :].rearrange("p k (j d) -> p (k j) d", d=P)[:, 0:sum(SCALED), :]
                            for b in range(2))
        q2_groups = q2_int[:, :, :].rearrange("p g (n d) -> p g n d", n=KC)
        assert FC * D == 2 * KC * TILE
        xn = q2_int[:, :, :].bitcast(F32).rearrange("p g d -> p (g d)")\
            .rearrange("p (b k n) -> p b k n", b=2, k=KC)
        xn_hi, xn_lo = h_hi, h_lo
        a_sb, b_sb, c_sb = u_sb[0:N, :, :], y_sb[0:N, 0:2, :], g_full[0:N, :, :]
        drive, state = y_sb[0:N, 2:4, :], z_acc[0:N, 0, :, :]
        scratch = q1_int[:, :, :].bitcast(F32).rearrange("p k f -> p (k f)").rearrange("p (b n) -> p b n", n=TILE)
        c_part, c_sum, cs_full = (scratch[0:N, i, :] for i in range(3))
        cs_parts = sb("cs_parts", [P, 2, TILE], F32R)
        raw = resid[:, NT - 1, :, :].rearrange("p a d -> p (a d)")
        bias_raw = raw[0:N, 0:2 * D].rearrange("p (b d) -> p b d", b=2)
        wy_raw = raw[:, 2 * D:3 * D]
        wc_raw = raw[:, 3 * D:3 * D + KC * N].rearrange("p (k n) -> p k n", k=KC)

        ps_fc1 = ctx.enter_context(nc.psum_tensor("ps_fc1", [P, 2, KC, TILE], F32))
        ps_z = ctx.enter_context(nc.psum_tensor("ps_z", [P, 3, TILE], F32))
        ps_tr = ctx.enter_context(nc.psum_tensor("ps_tr", [P, TILE], F32))
        ps_tr2 = ps_z[:, 2, :]
        back_banks = (ps_tr[:, :], ps_fc1[:, 0, 0, :])
        ps_ab = ps_z[:, 0, :]
        ps_c = ps_z[:, 1, :]
        ps_mix = ps_fc1

        x_loaded = [sem("x_loaded_even"), sem("x_loaded_odd")]
        rows_zero = sem("rows_zero")
        rows_loaded = sem("rows_loaded")
        mixer_rows_loaded = sem("mixer_rows_loaded")
        q1_loaded = sem("q1_loaded")
        q2_loaded = sem("q2_loaded")
        mixer_loaded = sem("mixer_loaded")
        ident_zero = sem("ident_zero")
        consts_ready = sem("consts_ready")
        rows_turned = sem("rows_turned")
        cols_ready = sem("cols_ready")
        q1_ready = sem("q1_ready")
        q2_ready = sem("q2_ready")
        s2_loaded = sem("s2_loaded")
        w2_int_ready = sem("w2_int_ready")
        w2_full_ready = sem("w2_full_ready")
        w2_hi_ready = sem("w2_hi_ready")
        w2_ready = sem("w2_ready")
        largest_found = sem("largest_found")
        largest_turned = sem("largest_turned")
        flag_ready = sem("flag_ready")
        wide_full = sem("wide_full")
        wide_ready = sem("wide_ready")
        raw_zero = sem("raw_zero")
        mixer_rounded = sem("mixer_rounded")
        mixer_ready = sem("mixer_ready")
        stored = sem("stored")
        stats_done = sem("stats_done")
        aggr_done = sem("aggr_done")
        var_ready = sem("var_ready")
        rstd_ready = sem("rstd_ready")
        res_terms = sem("res_terms")
        xhat_ready = sem("xhat_ready")
        resid_scaled = sem("resid_scaled")
        turned = sem("turned")
        turned_out = sem("turned_out")
        h_hi_ready = sem("h_hi_ready")
        h_ready = sem("h_ready")
        fc1_done = sem("fc1_done")
        u_ready = sem("u_ready")
        y_ready = sem("y_ready")
        g_hi_ready = sem("g_hi_ready")
        g_ready = sem("g_ready")
        fc2_done = sem("fc2_done")
        z_added = [sem(f"z{n}_added") for n in range(KC)]
        back_done = sem("back_done")
        ffn_added = sem("ffn_added")
        ab_done = sem("ab_done")
        c_done = sem("c_done")
        a_ready = sem("a_ready")
        b_ready = sem("b_ready")
        c_part_ready = sem("c_part_ready")
        c_sum_ready = sem("c_sum_ready")
        c_ready = sem("c_ready")
        drive_ready = sem("drive_ready")
        state_ready = sem("state_ready")
        cs_ready = sem("cs_ready")
        cs_hi_ready = sem("cs_hi_ready")
        cs_lo_ready = sem("cs_lo_ready")
        xn_ready = sem("xn_ready")
        mix_done = sem("mix_done")
        mix_added = sem("mix_added")

        def col(r):
            return cols[:, r:r + 1]

        def wait(eng, signal, count):
            if type(count) is not int or count > 0:
                eng.wait_ge(signal, count)

        def in_sum(g, n):
            return g in scaled_groups[n]

        def sum_ends(g, n):
            return g == scaled_groups[n][-1]

        def added_before(g, n):
            return max(g - SCALED[0] + 1, 0) if n == 0 else min(g, FC - SCALED[1])

        def groups_of(x, groups, n):
            return x[:, groups[n][0]:groups[n][-1] + 1, n, :]

        def bank_of(g, n, par):
            return ps_z[:, BANKS[par][n][g], :]

        def filled_before(bank, g, n, ff, par):
            here = [(j, m) for j in range(FC) for m in (FIRST[j], 1 - FIRST[j])]
            before = here[:here.index((g, n))] if g < FC else here
            for back, uses, p in ((0, before, par), (1, here, 1 - par)):
                for j, m in reversed(uses):
                    if BANKS[p][m][j] == bank:
                        return m, SUMS[m] * (ff - back) + (added_before(j, m) + 1)

        halves = (range(0, SUB // 2), range(SUB // 2, SUB))

        def over_tiles(eng, tile):
            tile(0, 0, 0, 2)
            tile(1, 1, 1, 2)
            with eng.Fori(0, PAIRS) as i:
                tile(2 * i + 2, 0, 2, 2)
                tile(2 * i + 3, 1, 2, 2)
            tile(NT - 2, 0, 2, 1)
            tile(NT - 1, 1, 2, 0)

        block = ctx.enter_context(nc.Block())

        @block.sync
        def _(sp):
            sp.dma_start(resid[:, 0, :, :], x_view[:, 0, :, :]).then_inc(x_loaded[0], 16)
            sp.wait_ge(rows_zero, 1)
            small = [(s1.rearrange("k (c p) -> (k c) p", p=P), R_S1, KC * FC),
                     (b1.rearrange("(c p) -> c p", p=P), R_B1, FC),
                     (s2.rearrange("g (n p) -> (g n) p", p=P), R_S2, FC * KC),
                     (b2.rearrange("(n p) -> n p", p=P), R_B2, KC),
                     (gamma.rearrange("(k p) -> k p", p=P), R_GAMMA, KC),
                     (beta.rearrange("(k p) -> k p", p=P), R_BETA, KC)]
            for src, r, n in small:
                sp.dma_start(rows[r:r + n, :], src).then_inc(rows_loaded, 16)
            for n in range(KC):
                scales = s2[scaled_groups[n][0]:scaled_groups[n][-1] + 1, n * P:(n + 1) * P]
                sp.dma_start(s2_wide[:, scaled_place[n], :], scales.rearrange("(o j) d -> o j d", o=1).broadcast_to(
                    [P, SCALED[n], P])).then_inc(s2_loaded, 16)
            sp.dma_start(resid[:, 1, :, :], x_view[:, 1, :, :]).then_inc(x_loaded[1], 16)
            for dst, src in ((wab_sb[:, :, 0:N], wa), (wab_sb[:, :, N:2 * N], wb), (wc_raw, wc),
                             (wd_sb[:, :, :], wd)):
                sp.dma_start(dst, src.rearrange("(k p) n -> p k n", p=P)).then_inc(mixer_loaded, 16)
            sp.wait_ge(raw_zero, 1)
            for at in (0, N):
                sp.dma_start(wy_raw[at:at + N, :], wy).then_inc(mixer_loaded, 16)
            for at in (0, 32):
                for i, v in enumerate((by, bd)):
                    bias = v.rearrange("(a b n) -> a b n", a=1, b=1).broadcast_to([1, 2, D])
                    sp.dma_start(bias_raw[at + i:at + i + 1, :, :], bias).then_inc(mixer_loaded, 16)
            with sp.Fori(0, NT // 2 - 2) as i:
                for par in range(2):
                    sp.wait_ge(x_loaded[par], 16 * i + 16)
                    sp.dma_start(resid[:, 2 * i + (2 + par), :, :],
                                 x_view[:, 2 * i + (2 + par), :, :]).then_inc(x_loaded[par], 16)
            sp.wait_ge(mixer_ready, 1)
            for par in range(2):
                sp.wait_ge(x_loaded[par], 8 * NT - 16)
                sp.dma_start(resid[:, NT - 2 + par, :, :],
                             x_view[:, NT - 2 + par, :, :]).then_inc(x_loaded[par], 16)

            with sp.Fori(0, NT) as t:
                sp.wait_ge(ffn_added, 2 * t + (2 * NT + 2))
                sp.dma_start(out_view[:, t, :, :], resid[:, t, :, :]).then_inc(stored, 16)
            sp.wait_ge(stored, 16 * NT)

        @block.gpsimd
        def _(pool):
            nc.gpsimd.memset(rows[:, :], 0.0).then_inc(rows_zero, 1)
            nc.gpsimd.memset(ident[:, :], 0.0).then_inc(ident_zero, 1)
            pool.wait_ge(ident_zero, 1)
            nc.gpsimd.affine_select(out=ident[:, :], in_=ident[:, :], compare_op=ALU.not_equal, fill=1.0,
                                    base=0, pattern=[[-1, P]], channel_multiplier=1).then_inc(consts_ready, 1)
            pool.wait_ge(consts_ready, 1)
            nc.gpsimd.memset(minus_half[:, :], -0.5).then_inc(consts_ready, 1)
            pool.wait_ge(consts_ready, 2)
            nc.gpsimd.memset(bias_raw, 0.0).then_inc(raw_zero, 1)
            for v, r, at in ((ba, R_AB, 0), (bb, R_AB, N), (bc, R_C, N)):
                pool.dma_start(rows[r:r + 1, at:at + N],
                               v.rearrange("(a n) -> a n", a=1)).then_inc(mixer_rows_loaded, 16)

            def rsqrt(ln, n):
                pool.wait_ge(var_ready, ln + 1)
                nc.gpsimd.tensor_tensor(rstd[:, 0:n], var_terms[:, 0:n], minus_half[:, 0:n],
                                        ALU.pow).then_inc(rstd_ready, 1)

            def h_low(ln, ff, par, c):
                pool.wait_ge(h_hi_ready, 2 * ff + (c + 1))
                wait(pool, fc1_done, FC * ff - FC)
                nc.gpsimd.tensor_tensor(h_lo[:, par, c, :], h_full[:, c, :], h_hi[:, par, c, :].bitcast(F32),
                                        ALU.subtract).then_inc(h_ready, 1)

            def g_low(step, slot):
                pool.wait_ge(g_hi_ready, step + 1)
                wait(pool, fc2_done, 2 * step - 6)
                nc.gpsimd.tensor_tensor(g_lo[:, slot % 4, :], g_full[:, slot % 2, :],
                                        g_hi[:, slot % 4, :].bitcast(F32), ALU.subtract).then_inc(g_ready, 1)

            def xn_low(t, par, c):
                pool.wait_ge(turned_out, 2 * t + (2 * NT + c + 1))
                nc.gpsimd.tensor_tensor(xn_lo[:, par, c, :], xn[:, par, c, :], xn_hi[:, par, c, :].bitcast(F32),
                                        ALU.subtract).then_inc(xn_ready, 1)

            def cs_low(t, par):
                pool.wait_ge(cs_hi_ready, t + 1)
                if type(t) is int and t == NT - 1:
                    pool.wait_ge(h_ready, 2 * NT + 2)
                else:
                    pool.wait_ge(xn_ready, 2 * t + 4)
                nc.gpsimd.tensor_tensor(cs_parts[N:2 * N, par, :], cs_full, cs_parts[0:N, par, :].bitcast(F32),
                                        ALU.subtract).then_inc(cs_lo_ready, 1)
                pool.wait_ge(cs_lo_ready, t + 1)

            def feed_forward(ff0, ln0):
                def tile(t, par, before, behind):
                    ff, ln = t + ff0, t + ln0
                    for f in range(FC):
                        if before or f >= 1:
                            g_low(FC * ff + (f - 1), f + 7)
                        if behind >= 1 and f in LOWER_PART_AT[not before]:
                            h_low(ln + 1, ff + 1, 1 - par, LOWER_PART_AT[not before].index(f))
                        elif ff0 == 0 and f in LOWER_PART_AT[not before]:
                            xn_low(0, 0, LOWER_PART_AT[not before].index(f))
                        if f == RSQRT_AT and (behind >= 2 or ff0 == 0):
                            rsqrt(ln + 2, 2 * SUB if behind >= 2 else SUB)
                if ff0 == 0:
                    rsqrt(ln0, 2 * SUB)
                    for c in range(KC):
                        h_low(ln0, ff0, 0, c)
                    pool.wait_ge(s2_loaded, 16 * KC)
                    pool.wait_ge(w2_int_ready, KC)
                    nc.gpsimd.tensor_tensor(w2_full, w2_full, s2_wide, ALU.mult).then_inc(w2_full_ready, 1)
                    rsqrt(ln0 + 1, 2 * SUB)
                    pool.wait_ge(w2_hi_ready, 1)
                    nc.gpsimd.tensor_tensor(w2_lo[:, :, :], w2_full, w2_hi[:, :, :].bitcast(F32),
                                            ALU.subtract).then_inc(w2_ready, 1)
                over_tiles(pool, tile)
                g_low(FC * (ff0 + NT) - 1, 7)

            feed_forward(0, 0)

            def mixer_tile(t, par, before, behind):
                if before:
                    cs_low(t - 1, 1 - par)
                rsqrt(t + (NT + 2), SUB if behind >= 2 else 2 * SUB)
                for c in range(KC):
                    if behind:
                        xn_low(t + 1, 1 - par, c)
                    else:
                        h_low(2 * NT, NT, 0, c)
            over_tiles(pool, mixer_tile)
            cs_low(NT - 1, 1)

            feed_forward(NT, 2 * NT)

        @block.scalar
        def _(act):
            act.dma_start(q1_int[:, :, :], q1.rearrange("(k p) f -> p k f", p=P)).then_inc(q1_loaded, 16)
            act.dma_start(q2_int[:, :, :], q2.rearrange("(g p) d -> p g d", p=P)).then_inc(q2_loaded, 16)
            act.wait_ge(consts_ready, 2)
            nc.scalar.activation(silu_table[:, :], minus_half[:, 0:1], ACT.Silu)
            act.wait_ge(q1_loaded, 16)
            nc.scalar.activation(q1_sb[:, :, :], q1_int[:, :, :], ACT.Copy, bias=-ZERO_POINT).then_inc(q1_ready, 1)
            act.wait_ge(rows_turned, 1)
            nc.scalar.activation(cols[:, :], ps_tr2[:, 0:ROWS], ACT.Copy).then_inc(cols_ready, 1)
            act.wait_ge(q2_loaded, 16)
            for n in range(KC):
                nc.scalar.activation(q2_sb[:, whole_place[n], :], groups_of(q2_groups, whole_groups, n),
                                     ACT.Copy, bias=-ZERO_POINT).then_inc(q2_ready, 1)
            act.wait_ge(cols_ready, 1)

            def affine(ln, ff, par, c, outs=(0, 1), bank=ps_tr):
                if 0 in outs:
                    act.wait_ge(turned, 2 * ln + (c + 1))
                    wait(act, h_ready, 2 * ff + (c - 1))
                    nc.scalar.activation(h_full[:, c, :], bank[:, :], ACT.Identity, bias=col(R_BETA + c),
                                         scale=col(R_GAMMA + c)).then_inc(turned_out, 1)
                if 1 in outs:
                    act.wait_ge(turned_out, 2 * ln + (c + 1))
                    wait(act, fc1_done, FC * ff - FC)
                    nc.scalar.activation(h_hi[:, par, c, :], h_full[:, c, :], ACT.Copy).then_inc(h_hi_ready, 1)

            def first_group(step, f):
                act.wait_ge(fc1_done, step + 1)
                wait(act, y_ready, step - 1)
                nc.scalar.activation(u_sb[:, f % 2, :], ps_fc1[:, f % 2, 0, :], ACT.Identity,
                                     bias=col(R_B1 + f), scale=col(R_S1 + f)).then_inc(u_ready, 1)

            def first_sum(step, ff, par):
                act.wait_ge(fc2_done, 2 * step + (1 + FIRST[SCALED[0] - 1]))
                wait(act, back_done, 2 * ff - 2)
                nc.scalar.activation(z_acc[:, par, 0, :], bank_of(SCALED[0] - 1, 0, par), ACT.Identity,
                                     bias=col(R_B2)).then_inc(z_added[0], 1)

            def silu(step, slot):
                act.wait_ge(y_ready, step + 1)
                wait(act, g_ready, step - 1)
                nc.scalar.activation(g_full[:, slot % 2, :], y_sb[:, slot % 4, :], ACT.Silu)
                wait(act, fc2_done, 2 * step - 6)
                nc.scalar.activation(g_hi[:, slot % 4, :], y_sb[:, slot % 4, :],
                                     ACT.Silu).then_inc(g_hi_ready, 1)

            def turn_out(t, par, c, outs=(0, 1), bank=ps_tr):
                if 0 in outs:
                    act.wait_ge(turned, 2 * t + (2 * NT + c + 1))
                    nc.scalar.activation(xn[:, par, c, :], bank[:, :], ACT.Copy)
                if 1 in outs:
                    if type(t) is int and t < 2:
                        act.wait_ge(fc1_done, FC * (NT - 1 + t))
                    nc.scalar.activation(xn_hi[:, par, c, :], bank[:, :], ACT.Copy).then_inc(turned_out, 1)

            def feed_forward(ff0, ln0):
                def tile(t, par, before, behind):
                    ff, ln = t + ff0, t + ln0
                    for f in range(FC):
                        first_group(FC * ff + f, f)
                        if before or f >= 1:
                            silu(FC * ff + (f - 1), f + 7)
                        if behind and f in TURN_OUT_AT[not before]:
                            c, rounded = divmod(TURN_OUT_AT[not before].index(f), 2)
                            affine(ln + 1, ff + 1, 1 - par, c, (rounded,))
                        elif ff0 == 0 and f in TURN_OUT_AT[not before]:
                            c, rounded = divmod(TURN_OUT_AT[not before].index(f), 2)
                            turn_out(0, 0, c, (rounded,))
                        if f - LAG == SCALED[0] - 1:
                            first_sum(FC * ff + (f - LAG), ff, par)
                if ff0 == 0:
                    for c in range(KC):
                        affine(ln0, ff0, 0, c, bank=(ps_tr, ps_tr2)[c])
                    for n in range(KC):
                        nc.scalar.activation(w2_full[:, scaled_place[n], :],
                                             groups_of(q2_groups, scaled_groups, n), ACT.Copy,
                                             bias=-ZERO_POINT).then_inc(w2_int_ready, 1)
                over_tiles(act, tile)
                silu(FC * (ff0 + NT) - 1, 7)

            feed_forward(0, 0)

            def mixer_tile(t, par, before, behind):
                act.wait_ge(ab_done, t + 1)
                nc.scalar.activation(a_sb[:, par, :], ps_ab[0:N, :], ACT.Sigmoid,
                                     bias=cols[0:N, R_AB:R_AB + 1]).then_inc(a_ready, 1)
                nc.scalar.activation(b_sb[:, par, :], ps_ab[N:2 * N, :], ACT.Identity,
                                     bias=cols[N:2 * N, R_AB:R_AB + 1]).then_inc(b_ready, 1)
                act.wait_ge(c_done, t + 1)
                nc.scalar.activation(c_part, ps_c[N:2 * N, :], ACT.Identity,
                                     bias=cols[N:2 * N, R_C:R_C + 1]).then_inc(c_part_ready, 1)
                for c in range(KC) if before else ():
                    if behind:
                        turn_out(t + 1, 1 - par, c, bank=(ps_tr, ps_tr2)[c])
                    else:
                        affine(2 * NT, NT, 0, c, bank=(ps_tr, ps_tr2)[c])
                act.wait_ge(c_sum_ready, t + 1)
                nc.scalar.activation(c_sb[:, par, :], c_sum, ACT.Tanh).then_inc(c_ready, 1)
                if not behind:
                    nc.scalar.activation(silu_table[:, :], minus_half[:, 0:1], ACT.Silu)
                act.wait_ge(cs_ready, t + 1)
                wait(act, mix_done, 2 * t - 2)
                nc.scalar.activation(cs_parts[0:N, par, :], cs_full, ACT.Copy).then_inc(cs_hi_ready, 1)
            for c in range(KC):
                turn_out(1, 1, c)
            over_tiles(act, mixer_tile)

            feed_forward(NT, 2 * NT)

        @block.vector
        def _(dve):
            def statistics(t, blocks=range(SUB)):
                for a in blocks:
                    last = nc.vector.bn_stats(stats[:, a, :], resid[:, t, a, :])
                if blocks[-1] == SUB - 1:
                    last.then_inc(stats_done, 1)

            def variance(ln, twice):
                dve.wait_ge(stats_done, ln + 1)
                nc.vector.memset(wait_holder[:, :], 0.0)
                for a in range(SUB):
                    last = nc.vector.bn_aggr(mean_var[:, a, :], stats[:, a, :])
                last.then_inc(aggr_done, 1)
                dve.wait_ge(aggr_done, ln + 1)
                last = nc.vector.tensor_scalar(var_terms[:, 0:SUB], mean_var[:, :, 1], EPS, None, ALU.add)
                if twice:
                    last = nc.vector.tensor_scalar(var_terms[:, SUB:2 * SUB], mean_var[:, :, 1], 1.0 + EPS,
                                                   EPS * EPS, ALU.mult, ALU.add)
                last.then_inc(var_ready, 1)

            def normalise(ln, t, twice, blocks=range(SUB)):
                if blocks[0] == 0:
                    dve.wait_ge(rstd_ready, ln + 1)
                    wait(dve, turned, 2 * ln)
                at = SUB if twice else 0
                for a in blocks:
                    last = nc.vector.tensor_scalar(xhat[:, a, :], resid[:, t, a, :], mean_var[:, a, 0:1],
                                                   rstd[:, at + a:at + a + 1], ALU.subtract, ALU.mult)
                if blocks[-1] == SUB - 1:
                    last.then_inc(xhat_ready, 1)

            def residual(ff, t, blocks=range(SUB)):
                if blocks[0] == 0:
                    nc.vector.tensor_scalar(res_scale[:, :], rstd[:, 0:SUB], 0.5, 1.0, ALU.mult, ALU.add)
                    nc.vector.scalar_tensor_tensor(out=res_shift[:, :], in0=mean_var[:, :, 0], scalar=-0.5,
                                                   in1=rstd[:, 0:SUB], op0=ALU.mult,
                                                   op1=ALU.mult).then_inc(res_terms, 1)
                    dve.wait_ge(res_terms, ff + 1)
                for a in blocks:
                    last = nc.vector.tensor_scalar(resid[:, t, a, :], resid[:, t, a, :], res_scale[:, a:a + 1],
                                                   res_shift[:, a:a + 1], ALU.mult, ALU.add)
                if blocks[-1] == SUB - 1:
                    last.then_inc(resid_scaled, 1)

            def second_group(step, f):
                dve.wait_ge(u_ready, step + 1)
                wait(dve, g_hi_ready, step - 3)
                nc.vector.scalar_tensor_tensor(out=y_sb[:, f % 4, :], in0=ps_fc1[:, f % 2, 1, :],
                                               scalar=col(R_S1 + FC + f), in1=u_sb[:, f % 2, :],
                                               op0=ALU.mult, op1=ALU.add).then_inc(y_ready, 1)

            def add_group(step, ff, g, par, turns=range(KC)):
                for turn in turns:
                    n = abs(FIRST[g] - turn)
                    if in_sum(g, n) and (n == 0 or not sum_ends(g, n)):
                        continue
                    dve.wait_ge(fc2_done, 2 * step + (turn + 1))
                    z, bank, scale = z_acc[:, par, n, :], bank_of(g, n, par), col(R_S2 + KC * g + n)
                    if added_before(g, n) == 0:
                        wait(dve, back_done, 2 * ff - 2)
                    else:
                        dve.wait_ge(z_added[n], SUMS[n] * ff + added_before(g, n))
                    if in_sum(g, n):
                        op = nc.vector.tensor_tensor(z, bank, z, ALU.add)
                    elif added_before(g, n) == 0:
                        op = nc.vector.tensor_scalar(z, bank, scale, col(R_B2 + n), ALU.mult, ALU.add)
                    else:
                        op = nc.vector.scalar_tensor_tensor(out=z, in0=bank, scalar=scale, in1=z,
                                                            op0=ALU.mult, op1=ALU.add)
                    op.then_inc(z_added[n], 1)

            def add_ffn(ff, t, half, bank=back_banks[0]):
                dve.wait_ge(back_done, 2 * ff + (half + 1))
                dve.wait_ge(resid_scaled, ff + 1)
                part = resid[:, t, 2 * half:2 * half + 2, :]
                nc.vector.scalar_tensor_tensor(out=part, in0=bank.rearrange("p (a d) -> p a d", a=2),
                                               scalar=0.25, in1=part, op0=ALU.mult,
                                               op1=ALU.add).then_inc(ffn_added, 1)

            def feed_forward(ff0, ln0):
                def tile(t, par, before, behind):
                    ff, ln = t + ff0, t + ln0
                    for f in range(FC):
                        here = f >= LAG
                        group = (FC * ff + (f - LAG), ff if here else ff - 1, (f - LAG) % FC,
                                 par if here else 1 - par)
                        if before or here:
                            add_group(*group, range(1))
                        second_group(FC * ff + f, f)
                        if before or here:
                            add_group(*group, range(1, KC))
                        if ff0 and not before and f == 0:
                            for half in range(2):
                                add_mixer(NT - 1, 1, half)
                        if behind >= 1 and f == 0:
                            residual(ff + 1, t + 1, range(2, SUB))
                        if ff0 == 0 and not before and f == 3:
                            prepare_mixer()
                        if behind >= 2 or ff0 == 0:
                            t2, twice = (t + 2, True) if behind >= 2 else (1 - behind, False)
                            if f == STATISTICS_AT[0] and twice and ff0 == 0:
                                dve.wait_ge(x_loaded[par], 8 * t + (32 if par == 0 else 24))
                            if f in STATISTICS_AT:
                                statistics(t2, halves[STATISTICS_AT.index(f)])
                            if f == VARIANCE_AT:
                                variance(ln + 2, twice)
                            if f in NORMALISE_AT[not before]:
                                normalise(ln + 2, t2, twice, halves[NORMALISE_AT[not before].index(f)])
                            if f == RESIDUAL_AT[not before] and twice:
                                residual(ff + 2, t + 2, range(2))
                        if before and f in ADD_AT:
                            add_ffn(ff - 1, t - 1, ADD_AT.index(f))

                if ff0 == 0:
                    dve.wait_ge(x_loaded[0], 16)
                    statistics(0)
                    variance(ln0, True)
                    normalise(ln0, 0, True)
                    largest_of(0, q1_sb, q1_ready, 1)
                    largest_of(1, q2_sb, q2_ready, KC)
                    find_width()
                    residual(ff0, 0)
                    dve.wait_ge(x_loaded[1], 16)
                    statistics(1)
                    variance(ln0 + 1, True)
                    dve.wait_ge(w2_full_ready, 1)
                    nc.vector.tensor_copy(w2_hi[:, :, :], w2_full).then_inc(w2_hi_ready, 1)
                    normalise(ln0 + 1, 1, True)
                    residual(ff0 + 1, 1, range(2))
                over_tiles(dve, tile)
                end = ff0 + NT
                if ff0 == 0:
                    statistics(2)
                    variance(NT + 2, False)
                for f in range(LAG):
                    add_group(FC * end + f - LAG, end - 1, FC + f - LAG, 1)
                for half in range(2):
                    add_ffn(end - 1, NT - 1, half, back_banks[half if ff0 else 0])

            def prepare_mixer():
                nc.vector.tensor_scalar(ones[:, :], ident[0:N, :], 0.0, 1.0, ALU.mult, ALU.add)
                dve.wait_ge(mixer_loaded, 16 * 10)
                nc.vector.tensor_copy(wc_parts[:, :, 0, :], wc_raw)
                nc.vector.tensor_copy(wy_hi[:, :], wy_raw)
                nc.vector.tensor_copy(bias_parts[:, :, :], bias_raw).then_inc(mixer_rounded, 1)
                dve.wait_ge(mixer_rounded, 1)
                nc.vector.tensor_tensor(wc_parts[:, :, 1, :], wc_raw, wc_parts[:, :, 0, :].bitcast(F32),
                                        ALU.subtract)
                nc.vector.tensor_tensor(wy_lo[:, :], wy_raw, wy_hi[:, :].bitcast(F32), ALU.subtract)
                nc.vector.tensor_tensor(bias_parts[32:34, :, :], bias_raw[32:34, :, :],
                                        bias_parts[32:34, :, :].bitcast(F32),
                                        ALU.subtract).then_inc(mixer_ready, 1)

            def add_mixer(t, par, half):
                dve.wait_ge(mix_done, 2 * t + (half + 1))
                part = resid[:, t, 2 * half:2 * half + 2, :]
                nc.vector.tensor_tensor(part, ps_mix[:, par, half, :].rearrange("p (a d) -> p a d", a=2), part,
                                        ALU.add).then_inc(mix_added, 1)

            def largest_of(i, q, ready, count):
                dve.wait_ge(ready, count)
                nc.vector.tensor_reduce(out=largest[:, i:i + 1], in_=q[:, :, :].bitcast(F32), axis=AX.XY,
                                        op=ALU.max, apply_absolute_value=True).then_inc(largest_found, 1)

            def find_width():
                dve.wait_ge(largest_found, 2)
                nc.vector.tensor_reduce(out=largest[:, 2:3], in_=largest[:, 0:2], axis=AX.X,
                                        op=ALU.max).then_inc(largest_found, 1)
                dve.wait_ge(largest_turned, 1)
                nc.vector.tensor_reduce(out=largest[0:1, 3:4], in_=ps_z[0:1, 0, 0:P], axis=AX.X,
                                        op=ALU.max).then_inc(largest_found, 1)
                dve.wait_ge(largest_found, 4)
                nc.vector.tensor_scalar(wide_flag[:, :], largest[0:1, 3:4], WIDE, None,
                                        ALU.is_ge).then_inc(flag_ready, 1)
                dve.wait_ge(flag_ready, 1)
                wide = dve.value_load(wide_flag[0:1, 0:1], min_val=0, max_val=1)
                with dve.If(wide > 0):
                    chunks = [(q1_low[:, k, :], q1_sb[:, k, :], q1_int[:, k, :]) for k in range(KC)]
                    chunks += [(q2_low[:, whole_place[n], :], q2_sb[:, whole_place[n], :],
                                groups_of(q2_groups, whole_groups, n)) for n in range(KC)]
                    for i, (low, high, whole) in enumerate(chunks):
                        nc.vector.tensor_scalar(whole.bitcast(F32), whole, -ZERO_POINT, None,
                                                ALU.add).then_inc(wide_full, 1)
                        dve.wait_ge(wide_full, i + 1)
                        nc.vector.tensor_tensor(low, whole.bitcast(F32), high.bitcast(F32),
                                                ALU.subtract).then_inc(wide_ready, 1)

            feed_forward(0, 0)

            def scan(t, par):
                dve.wait_ge(b_ready, t + 1)
                nc.vector.scalar_tensor_tensor(out=drive[:, par, :], in0=a_sb[:, par, :], scalar=1.0,
                                               in1=b_sb[:, par, :], op0=ALU.subtract,
                                               op1=ALU.mult).then_inc(drive_ready, 1)
                dve.wait_ge(drive_ready, t + 1)
                nc.vector.tensor_tensor_scan(state[:, par, :], a_sb[:, par, :], drive[:, par, :],
                                             state[:, 0, TILE - 1:TILE] if par else 0.0,
                                             ALU.mult, ALU.subtract).then_inc(state_ready, 1)

            def mixer_tile(t, par, before, behind):
                twice = behind < 2
                t2 = 1 - behind if twice else t + 2
                if before:
                    statistics(t2)
                    variance(t + (NT + 2), twice)
                scan(t, par)
                dve.wait_ge(c_part_ready, t + 1)
                nc.vector.tensor_tensor(c_sum, ps_c[0:N, :], c_part, ALU.add).then_inc(c_sum_ready, 1)
                def norm():
                    normalise(t + (NT + 2), t2, twice)
                    if twice:
                        residual(NT + t2, t2, range(2 if t2 else SUB))

                if behind:
                    norm()
                if before:
                    for half in range(2):
                        add_mixer(t - 1, 1 - par, half)
                dve.wait_ge(state_ready, t + 1)
                dve.wait_ge(c_ready, t + 1)
                wait(dve, cs_lo_ready, t)
                nc.vector.tensor_tensor(cs_full, c_sb[:, par, :], state[:, par, :], ALU.mult).then_inc(cs_ready, 1)
                if not behind:
                    norm()

            over_tiles(dve, mixer_tile)

            feed_forward(NT, 2 * NT)

        @block.tensor
        def _(pe):
            pe.wait_ge(consts_ready, 1)
            pe.wait_ge(rows_loaded, 16 * 6)
            pe.wait_ge(mixer_rows_loaded, 16 * 3)
            nc.tensor.transpose(ps_tr2[:, 0:ROWS], rows[:, :], ident[0:ROWS, 0:ROWS]).then_inc(rows_turned, 1)

            def turn(ln, c, bank=ps_tr, banks=1):
                pe.wait_ge(xhat_ready, ln + 1)
                wait(pe, turned_out, 2 * ln + (c - banks + 1))
                for a in range(SUB):
                    last = nc.tensor.transpose(bank[:, a * P:(a + 1) * P], xhat[:, a, c * P:(c + 1) * P],
                                               ident[:, :])
                last.then_inc(turned, 1)

            def products(out, pairs, start=True, stop=True):
                for i, (w, v) in enumerate(pairs):
                    last = nc.tensor.matmul(out, w, v, start=start and i == 0, stop=stop and i == len(pairs) - 1)
                return last

            def fc1(step, ff, f, par):
                if f == 0:
                    pe.wait_ge(h_ready, 2 * ff + 2)
                wait(pe, y_ready, step - 1)
                for k in range(KC):
                    last = products(ps_fc1[:, f % 2, k, :],
                                    [(w[:, k, f * P:(f + 1) * P], h[:, par, k, :])
                                     for w in q1_parts for h in (h_hi, h_lo)])
                last.then_inc(fc1_done, 1)

            def fc2(step, ff, g, par):
                if type(step) is int and step == 0:
                    pe.wait_ge(w2_ready, 1)
                pe.wait_ge(g_ready, step + 1)
                for n in (FIRST[g], 1 - FIRST[g]):
                    scaled = in_sum(g, n)
                    first = not scaled or g == scaled_groups[n][0]
                    if first:
                        chunk, count = filled_before(BANKS[par][n][g], g, n, ff, par)
                        wait(pe, z_added[chunk], count)
                    parts, groups, place = ((w2_hi, w2_lo), scaled_groups, scaled_place) if scaled else \
                        (q2_parts, whole_groups, whole_place)
                    at = place[n].start + g - groups[n][0]
                    products(bank_of(g, n, par), [(w[:, at, :], v[:, g % 4, :]) for w in parts for v in (g_hi, g_lo)],
                             start=first, stop=not scaled or sum_ends(g, n)).then_inc(fc2_done, 1)

            def turn_back(ff, par, half, turns, bank=back_banks[0]):
                for n in range(KC):
                    pe.wait_ge(z_added[n], SUMS[n] * ff + SUMS[n])
                pe.wait_ge(turned_out, turns)
                wait(pe, ffn_added, 2 * ff + (half if bank is back_banks[0] else 0))
                for a in range(2):
                    at = (2 * half + a) * P
                    for n in range(KC):
                        last = nc.tensor.transpose(bank[:, a * D + n * P:a * D + (n + 1) * P],
                                                   z_acc[:, par, n, at:at + P], ident[:, :])
                last.then_inc(back_done, 1)

            def feed_forward(ff0, ln0):
                def tile(t, par, before, behind):
                    ff, ln = t + ff0, t + ln0
                    for f in range(FC):
                        fc1(FC * ff + f, ff, f, par)
                        if before or f >= LAG:
                            fc2(FC * ff + (f - LAG), ff if f >= LAG else ff - 1, (f - LAG) % FC,
                                par if f >= LAG else 1 - par)
                        if (behind or ff0 == 0) and f in TURN_AT[not before]:
                            if f == TURN_AT[not before][0]:
                                wait(pe, ffn_added, 2 * ff - 2)
                            turn(ln + 1, TURN_AT[not before].index(f))
                        if ff0 and not before and f == 0:
                            y_products(NT - 1, 1)
                            pe.wait_ge(mix_added, 2 * NT)
                        if before and f in TURN_BACK_AT:
                            turn_back(ff - 1, 1 - par, TURN_BACK_AT.index(f),
                                      2 * ln + (4 if behind or ff0 == 0 else 2))
                over_tiles(pe, tile)
                end = ff0 + NT
                for f in range(LAG):
                    fc2(FC * end + f - LAG, end - 1, FC + f - LAG, 1)
                    if ff0 == 0 and f < 2:
                        if f == 0:
                            pe.wait_ge(mixer_ready, 1)
                            pe.wait_ge(turned_out, 2 * NT + 2)
                            pe.wait_ge(y_ready, FC * NT - 1)
                        d_products(0, 0, f)
                        if f == 0:
                            pe.wait_ge(ffn_added, 2 * NT - 2)
                        turn(NT + 1, f)
                if ff0:
                    for half in range(2):
                        turn_back(end - 1, 1, half, 6 * NT, back_banks[half])

            def d_products(t, par, half):
                nc.tensor.matmul(ps_mix[:, par, half, :], ones[:, :],
                                 bias_parts[:, :, :].rearrange("p b d -> p (b d)"), start=True, stop=False,
                                 skip_group_check=True)
                for a in range(2):
                    at = (2 * half + a) * P
                    for k in range(KC):
                        nc.tensor.matmul(ps_mix[:, par, half, a * D:(a + 1) * D], xn[:, par, k, at:at + P],
                                         wd_sb[:, k, :], start=False, stop=False, skip_group_check=True)

            def y_products(t, par):
                pe.wait_ge(cs_lo_ready, t + 1)
                for a in range(SUB):
                    for w in (wy_hi, wy_lo):
                        mm = nc.tensor.matmul(ps_mix[:, par, a // 2, (a % 2) * D:(a % 2 + 1) * D],
                                              cs_parts[:, par, a * P:(a + 1) * P], w[:, :], start=False,
                                              stop=a % 2 == 1 and w is wy_lo, skip_group_check=True)
                    if a % 2:
                        mm.then_inc(mix_done, 1)

            def wait_bank(bank):
                chunk, count = filled_before(bank, FC, 0, NT - 1, 1)
                pe.wait_ge(z_added[chunk], count)

            def mixer_tile(t, par, before, behind):
                pe.wait_ge(turned_out, 2 * t + (2 * NT + 2))
                if before:
                    pe.wait_ge(b_ready, t)
                else:
                    wait_bank(0)
                products(ps_ab, [(wab_sb[:, k, :], xn[:, par, k, :]) for k in range(KC)]).then_inc(ab_done, 1)
                if not before:
                    turn_back(NT - 1, 1, 0, 2 * NT + 4)
                pe.wait_ge(xn_ready, 2 * t + 2)
                if before:
                    pe.wait_ge(c_sum_ready, t)
                else:
                    wait_bank(1)
                products(ps_c, [(wc_parts[:, k, :, :].rearrange("p b n -> p (b n)"), v[:, par, k, :])
                                for k in range(KC) for v in (xn_hi, xn_lo)]).then_inc(c_done, 1)
                if not before:
                    turn_back(NT - 1, 1, 1, 2 * NT + 4)
                    return
                if before == 1:
                    pe.wait_ge(ffn_added, 2 * NT)
                turn(t + (NT + 1), 0, ps_tr, before)
                turn(t + (NT + 1), 1, ps_tr2, 2)
                if before == 2:
                    y_products(t - 1, 1 - par)
                wait(pe, mix_added, 2 * t - 2)
                for half in range(2):
                    d_products(t, par, half)
                if before == 1:
                    y_products(t - 1, 1 - par)

            def program():
                feed_forward(0, 0)
                over_tiles(pe, mixer_tile)
                pe.wait_ge(mix_added, 2 * NT - 2)
                feed_forward(NT, 2 * NT)

            pe.wait_ge(cols_ready, 1)
            for c in range(KC):
                turn(0, c, (ps_tr, ps_tr2)[c], 2)
            pe.wait_ge(largest_found, 3)
            nc.tensor.transpose(ps_z[0:1, 0, 0:P], largest[:, 2:3], ident[:, :]).then_inc(largest_turned, 1)
            pe.wait_ge(cols_ready, 1)
            pe.wait_ge(flag_ready, 1)
            wide = pe.value_load(wide_flag[0:1, 0:1], min_val=0, max_val=1)
            with pe.If(wide > 0):
                q1_parts, q2_parts = (q1_sb, q1_low), (q2_sb, q2_low)
                pe.wait_ge(wide_ready, 2 * KC)
                program()
            with pe.Else():
                q1_parts, q2_parts = (q1_sb,), (q2_sb,)
                program()


_INS = ['L0_attn_x', 'L0_attn_Wa', 'L0_attn_ba', 'L0_attn_Wb', 'L0_attn_bb', 'L0_attn_Wc', 'L0_attn_bc',
        'L0_attn_Wd', 'L0_attn_bd', 'L0_attn_Wy', 'L0_attn_by', 'L0_ffn_ln_gamma', 'L0_ffn_ln_beta',
        'L0_ffn_fc1_q', 'L0_ffn_fc1_scales', 'L0_ffn_fc1_bias', 'L0_ffn_fc2_q', 'L0_ffn_fc2_scales',
        'L0_ffn_fc2_bias']


def kernel(**inputs):
    import numpy as _np
    import concourse.bacc as _bacc
    from concourse import mybir as _mybir
    from concourse.bass_utils import run_bass_kernel_spmd as _run

    nc = _bacc.Bacc("TRN2", target_bir_lowering=False, num_devices=1)
    arrays, args = {}, []
    for name in _INS:
        a = _np.ascontiguousarray(inputs[name])
        arrays[f"in_{name}"] = a
        args.append(nc.dram_tensor(f"in_{name}", a.shape, _mybir.dt.from_np(a.dtype), kind="ExternalInput").ap())
    shape = inputs['L0_attn_x'].shape
    out = nc.dram_tensor("out_x", shape, _mybir.dt.float32, kind="ExternalOutput").ap()
    macaron_kernel(nc, *args, out)
    r = _run(nc, [arrays], core_ids=[0])
    return r.results[0]["out_x"]
```
